# Optimizing a Trainium2 kernel written in Bass

```python
import numpy as np
import jax
import jax.numpy as jnp

def _softmax(x, axis=-1):
    return jax.nn.softmax(x, axis=axis)

def _gelu(x):
    return jax.nn.gelu(x, approximate=True)

def _silu(x):
    return jax.nn.silu(x)

def _sigmoid(x):
    return jax.nn.sigmoid(x)

def _layernorm(x, axis=-1, eps=1e-05):
    m = jnp.mean(x, axis=axis, keepdims=True)
    v = jnp.var(x, axis=axis, keepdims=True)
    return (x - m) / jnp.sqrt(v + eps)

def _scatter_add(tgt, idx, src, axis=0):
    return tgt.at[idx].add(src)

def _segment_sum(src, seg, n):
    return jax.ops.segment_sum(src, seg, n)
kernel_name = 'mk_macaron_d1_jaxref_r8_c6a4de'

def setup_inputs(seed: int=0):
    np.random.seed(seed)
    _w = jnp.asarray

    def _L0_attn_setup():
        import jax, jax.numpy as jnp
        import numpy as np
        EPS = 1e-05
        NUM_HEADS = 16

        def _linear_attention(x, Wq, Wk, Wv, Wo, bo):
            B, L, E = x.shape
            H = NUM_HEADS
            D = E // H
            q = (x @ Wq.T).reshape(B, L, H, D)
            k = (x @ Wk.T).reshape(B, L, H, D)
            v = (x @ Wv.T).reshape(B, L, H, D)
            phi_q = jax.nn.elu(q) + 1.0
            phi_k = jax.nn.elu(k) + 1.0
            pq = jnp.moveaxis(phi_q, 1, 0)
            pk = jnp.moveaxis(phi_k, 1, 0)
            vt = jnp.moveaxis(v, 1, 0)
            S0 = jnp.zeros((B, H, D, D), x.dtype)
            z0 = jnp.zeros((B, H, D), x.dtype)

            def step(carry, inp):
                S, z = carry
                pq_t, pk_t, v_t = inp
                S = S + pk_t[..., :, None] * v_t[..., None, :]
                z = z + pk_t
                num = jnp.einsum('bhd,bhde->bhe', pq_t, S)
                den = jnp.sum(pq_t * z, axis=-1, keepdims=True) + EPS
                return ((S, z), num / den)
            (_, _), out = jax.lax.scan(step, (S0, z0), (pq, pk, vt))
            out = jnp.moveaxis(out, 0, 1).reshape(B, L, E)
            return out @ Wo.T + bo
        key = jax.random.key(seed)
        ks = jax.random.split(key, 6)
        B, L, E = (4, 512, 128)
        s = 1.0 / np.sqrt(E)
        return {'x': jax.random.normal(ks[0], (B, L, E), jnp.float32), 'Wq': jax.random.normal(ks[1], (E, E), jnp.float32) * s, 'Wk': jax.random.normal(ks[2], (E, E), jnp.float32) * s, 'Wv': jax.random.normal(ks[3], (E, E), jnp.float32) * s, 'Wo': jax.random.normal(ks[4], (E, E), jnp.float32) * s, 'bo': jnp.zeros((E,), jnp.float32)}
    _L0_attn_in = _L0_attn_setup()

    def _L0_ffn_setup():
        import jax, jax.numpy as jnp
        import numpy as np
        NUM_EXPERTS = 8
        HIDDEN = 128
        FFN = 512
        BATCH = 2
        SEQ = 256
        key = jax.random.key(seed)
        k_x, k_g, k_u, k_d = jax.random.split(key, 4)
        scale_in = 1.0 / np.sqrt(HIDDEN)
        scale_mid = 1.0 / np.sqrt(FFN)
        return {'hidden_states': jax.random.normal(k_x, (BATCH, SEQ, HIDDEN), dtype=jnp.float32), 'Wg': jax.random.normal(k_g, (NUM_EXPERTS, HIDDEN, FFN), dtype=jnp.float32) * scale_in, 'Wu': jax.random.normal(k_u, (NUM_EXPERTS, HIDDEN, FFN), dtype=jnp.float32) * scale_in, 'Wd': jax.random.normal(k_d, (NUM_EXPERTS, FFN, HIDDEN), dtype=jnp.float32) * scale_mid}
    _L0_ffn_in = _L0_ffn_setup()
    _d = {'L0_attn_x': _L0_attn_in['x'], 'L0_attn_Wq': _L0_attn_in['Wq'], 'L0_attn_Wk': _L0_attn_in['Wk'], 'L0_attn_Wv': _L0_attn_in['Wv'], 'L0_attn_Wo': _L0_attn_in['Wo'], 'L0_attn_bo': _L0_attn_in['bo'], 'L0_ffn_Wg': _L0_ffn_in['Wg'], 'L0_ffn_Wu': _L0_ffn_in['Wu'], 'L0_ffn_Wd': _L0_ffn_in['Wd']}
    _x0 = _d['L0_attn_x']
    _d['L0_attn_x'] = jax.random.normal(jax.random.fold_in(jax.random.key(seed), 1), (8, 1024, 128), dtype=_x0.dtype)
    del _x0
    return _d

def reference(L0_attn_x, L0_attn_Wq, L0_attn_Wk, L0_attn_Wv, L0_attn_Wo, L0_attn_bo, L0_ffn_Wg, L0_ffn_Wu, L0_ffn_Wd):

    def _L0_attn_ref(x, Wq, Wk, Wv, Wo, bo):
        import jax, jax.numpy as jnp
        import numpy as np
        EPS = 1e-05
        NUM_HEADS = 16

        def _linear_attention(x, Wq, Wk, Wv, Wo, bo):
            B, L, E = x.shape
            H = NUM_HEADS
            D = E // H
            q = (x @ Wq.T).reshape(B, L, H, D)
            k = (x @ Wk.T).reshape(B, L, H, D)
            v = (x @ Wv.T).reshape(B, L, H, D)
            phi_q = jax.nn.elu(q) + 1.0
            phi_k = jax.nn.elu(k) + 1.0
            pq = jnp.moveaxis(phi_q, 1, 0)
            pk = jnp.moveaxis(phi_k, 1, 0)
            vt = jnp.moveaxis(v, 1, 0)
            S0 = jnp.zeros((B, H, D, D), x.dtype)
            z0 = jnp.zeros((B, H, D), x.dtype)

            def step(carry, inp):
                S, z = carry
                pq_t, pk_t, v_t = inp
                S = S + pk_t[..., :, None] * v_t[..., None, :]
                z = z + pk_t
                num = jnp.einsum('bhd,bhde->bhe', pq_t, S)
                den = jnp.sum(pq_t * z, axis=-1, keepdims=True) + EPS
                return ((S, z), num / den)
            (_, _), out = jax.lax.scan(step, (S0, z0), (pq, pk, vt))
            out = jnp.moveaxis(out, 0, 1).reshape(B, L, E)
            return out @ Wo.T + bo
        return _linear_attention(x, Wq, Wk, Wv, Wo, bo)

    def _L0_ffn_ref(hidden_states, Wg, Wu, Wd):
        import jax, jax.numpy as jnp
        import numpy as np
        NUM_EXPERTS = 8
        HIDDEN = 128
        FFN = 512
        BATCH = 2
        SEQ = 256
        B, S, H = hidden_states.shape
        x = hidden_states.reshape(-1, H)

        def expert_step(acc, w):
            wg, wu, wd = w
            h = jax.nn.silu(x @ wg) * (x @ wu)
            return (acc + h @ wd, None)
        acc, _ = jax.lax.scan(expert_step, jnp.zeros_like(x), (Wg, Wu, Wd))
        return acc.reshape(B, S, H)
    x = L0_attn_x
    x = x + 0.5 * _L0_ffn_ref(_layernorm(x, axis=-1), L0_ffn_Wg, L0_ffn_Wu, L0_ffn_Wd)
    x = x + _L0_attn_ref(_layernorm(x, axis=-1), L0_attn_Wq, L0_attn_Wk, L0_attn_Wv, L0_attn_Wo, L0_attn_bo)
    x = x + 0.5 * _L0_ffn_ref(_layernorm(x, axis=-1), L0_ffn_Wg, L0_ffn_Wu, L0_ffn_Wd)
    return x

_drawn_inputs = setup_inputs


def setup_inputs(seed=0):
    import zlib

    import numpy as np

    out = dict(_drawn_inputs(seed))
    spreads = {'L0_attn_bo': (0.0, 0.1)}
    factors = {'L0_attn_Wq': 4.188}
    for name, (base, spread) in spreads.items():
        noise = np.random.default_rng([zlib.crc32(name.encode()), seed]).standard_normal(out[name].shape)
        drawn = base * np.exp(spread * noise) if base else spread * noise
        out[name] = jnp.asarray(drawn.astype(out[name].dtype))
    for name, factor in factors.items():
        out[name] = (out[name] * factor).astype(out[name].dtype)
    return out
```

```python
from contextlib import ExitStack

import concourse.bass as bass
from concourse import mybir

P = 128
F32 = mybir.dt.float32
F16 = mybir.dt.float16
I32 = mybir.dt.int32
ALU = mybir.AluOpType
ACT = mybir.ActivationFunctionType
AX = mybir.AxisListType
RMAX = bass.bass_isa.ReduceOp.max

LN_EPS = 1e-5
ATT_EPS = 1e-5
HEADS = 16
W_EXP = 4
H_EXP = 2 * (7 + W_EXP + 1) - 15
LAG = 3


class Step:

    def __init__(self, engine, slot, signal, emit, after, inc=1):
        self.engine, self.slot, self.sem_name, self.emit = engine, slot, signal, emit
        self.use, self.value = None, None
        self.after, self.inc = [s for s in after if s is not None], inc


class Use:

    def __init__(self, start, end, index):
        self.start, self.end, self.index = start, end, index
        self.readers, self.before = [], None

    def free(self):
        return self.before.readers if self.before else []


class Ring:

    def __init__(self, n):
        self.uses = [[] for _ in range(n)]

    def take(self, start, length, fixed=False):
        while True:
            for index, uses in enumerate(self.uses):
                if all(u.end < start or u.start > start + length - 1 for u in uses):
                    use = Use(start, start + length - 1, index)
                    uses.append(use)
                    return use
            assert not fixed, "no buffer is free"
            start += 1

    def link(self):
        for uses in self.uses:
            uses.sort(key=lambda u: u.start)
            for a, b in zip(uses, uses[1:]):
                b.before = a


def macaron_program(nc, x_d, wq_d, wk_d, wv_d, wo_d, bo_d, wg_d, wu_d, wd_d, out_d):
    B, L, E = x_d.shape
    X, _, FF = wg_d.shape
    D = E // HEADS
    T = 512
    TT = T // P
    BB = L // T
    NB = B * BB
    SL = FF // P
    NC = X * SL
    assert E == P and BB == 2 and FF % P == 0 and L % T == 0

    order = [(1, 0), (1, 1), (1, 2)]
    for b in range(3, B):
        order += [(2, b - 3), (1, b)]
    order += [(2, b) for b in range(B - 3, B)]
    segs = [(f, b * BB + j) for f, b in order for j in range(BB)]
    seg_of = {fb: s for s, fb in enumerate(segs)}
    NU = len(segs) * NC

    ctx = ExitStack()
    with ctx:
        def sb(name, shape, dt=F32):
            return ctx.enter_context(nc.sbuf_tensor(name, shape, dt))

        wg_hi, wg_lo = sb("wg_hi", [P, NC * P], F16), sb("wg_lo", [P, NC * P], F16)
        wu_hi, wu_lo = sb("wu_hi", [P, NC * P], F16), sb("wu_lo", [P, NC * P], F16)
        wd_hi, wd_lo = sb("wd_hi", [P, NC * P], F16), sb("wd_lo", [P, NC * P], F16)
        x_tok = sb("x_tok", [P, NB * TT, E])
        n_raw = NC * P
        names = [("k_act", L), ("k_lin", L), ("q_act", L), ("q_lin", L), ("v_T", L), ("rden", L), ("num", L),
                 ("k_rep", 3 * L), ("q_rep", 3 * L), ("kv", 2 * T), ("state", 3 * T), ("qs", 3 * T)]
        arena = sb("arena", [P, max(3 * n_raw, sum(n for _, n in names))])
        raw = {w: arena[:, i * n_raw:(i + 1) * n_raw] for i, w in enumerate(("g", "u", "d"))}
        part, at = {}, 0
        for name, n in names:
            part[name] = arena[:, at:at + n]
            at += n
        silu_sb = sb("silu_sb", [P, 3, T])
        h_sb = sb("h_sb", [P, 3, T])
        NH = 5
        h_hi, h_lo = sb("h_hi", [P, NH, T], F16), sb("h_lo", [P, NH, T], F16)
        NX, NL = 3, 3
        xn_hi, xn_lo = sb("xn_hi", [P, NX, T], F16), sb("xn_lo", [P, NX, T], F16)
        down_sb = sb("down_sb", [P, 2, T])
        xn_tok = sb("xn_tok", [P, NL, T])
        xn_T = sb("xn_T", [P, T])
        stats = sb("stats", [P, NL, TT, 6])
        mean_var = sb("mean_var", [P, NL, TT, 2])
        var_eps = sb("var_eps", [P, NL, TT])
        rstd = sb("rstd", [P, NL, TT])
        minus_half = sb("minus_half", [P, TT])
        ident = sb("ident", [P, P])
        head_ones = sb("head_ones", [P, P])
        w_att = {w: sb(f"w{w}_raw", [P, P]) for w in "qkvo"}
        w_att_T = {w: sb(f"w{w}_T", [P, P]) for w in "qkvo"}
        bo_all = sb("bo_all", [P, P])
        scal = sb("scal", [P, 32])

        def col(i):
            return scal[:, i:i + 1]
        amax_part = {"g": col(0), "u": col(1), "d": col(2)}
        amax_part2 = {"g": col(3), "u": col(4), "d": col(5)}
        amax_row = {"g": col(6), "u": col(7), "d": col(8)}
        amax_all = {"g": col(9), "u": col(10), "d": col(11)}
        pow2 = {"g": col(12), "u": col(13), "d": col(14)}
        pow2_inv = {"g": col(15), "u": col(16), "d": col(17)}
        w_scale = {"g": col(18), "u": col(19), "d": col(20)}
        w_unscale = {"g": col(21), "u": col(22), "d": col(23)}
        pow2_raw = {"g": col(24), "u": col(25), "d": col(26)}
        h_scale, gu_unscale, out_scale = col(27), col(28), col(29)

        psum = [ctx.enter_context(nc.psum_tensor(f"bank{i}", [P, T], F32)) for i in range(8)]
        gate_ps, up_ps, down_ps, misc_ps = psum[0:2], psum[2:4], psum[4:6], psum[6:8]
        scratch = nc.dram_tensor("rep_scratch", (B, 2, P, L), F32, kind="Internal").ap()

        steps = []

        def step(engine, slot, signal, emit, after=(), inc=1):
            s = Step(engine, slot, signal, emit, after, inc)
            steps.append(s)
            return s

        misc = Ring(2)
        xn_ring, ln_ring = Ring(NX), Ring(NL)
        rep_ring = {"k": Ring(3), "q": Ring(3)}

        def dma(slot, signal, out, in_, after=()):
            return step("sync", slot, signal, lambda e: e.dma_start(out, in_), after, 16)

        V, S, G, TE = nc.vector, nc.scalar, nc.gpsimd, nc.tensor

        def on_dve(slot, signal, emit, after=()):
            return step("vector", slot, signal, lambda e: emit(), after)

        def on_act(slot, signal, emit, after=()):
            return step("scalar", slot, signal, lambda e: emit(), after)

        def on_pool(slot, signal, emit, after=()):
            return step("gpsimd", slot, signal, lambda e: emit(), after)

        def on_pe(slot, signal, emit, after=()):
            return step("tensor", slot, signal, lambda e: emit(), after)

        def on_pe_misc(slot, hold, signal, emit, after=()):
            use = misc.take(slot, hold)
            bank = misc_ps[use.index]
            s = step("tensor", use.start, signal, lambda e: emit(bank), after)
            s.use = use
            return s, use, bank

        x_rows = x_d.rearrange("b l e -> (b l) e")
        out_rows = out_d.rearrange("b l e -> (b l) e")

        def block_rows(rows, blk):
            return rows[blk * T:(blk + 1) * T, :].rearrange("(t p) e -> p t e", p=P)

        load_x = {}

        def load_block(blk, slot):
            load_x[blk] = dma(slot, f"x_in{blk}", x_tok[:, blk * TT:(blk + 1) * TT, :], block_rows(x_rows, blk))

        load_block(0, -60)
        half_x = X // 2
        load_w = {}
        for w, src in (("g", wg_d), ("u", wu_d)):
            for i in range(2):
                dst = raw[w][:, i * n_raw // 2:(i + 1) * n_raw // 2].rearrange("p (x f) -> p x f", f=FF)
                load_w[w, i] = dma(-59, f"w{w}_in{i}", dst,
                                   src[i * half_x:(i + 1) * half_x, :, :].rearrange("x e f -> e x f"))
        for i in range(2):
            dst = raw["d"][:, i * n_raw // 2:(i + 1) * n_raw // 2].rearrange("p (c e) -> p c e", e=E)
            load_w["d", i] = dma(-58, f"wd_in{i}", dst,
                                 wd_d[i * half_x:(i + 1) * half_x, :, :].rearrange("x (j p) e -> p (x j) e", p=P))
        load_block(1, -57)
        load_att = {w: dma(-56, f"w{w}_in", w_att[w][:, :], src)
                    for w, src in zip("qkvo", (wq_d, wk_d, wv_d, wo_d))}
        load_bo = dma(-56, "bo_in", bo_all[:, :], bo_d.rearrange("(a e) -> a e", a=1).to_broadcast([P, E]))
        for blk in range(2, NB):
            load_block(blk, -55)

        zero_id = on_pool(-60, "pool_const", lambda: G.memset(ident[:, :], 0.0))
        one_head = on_pool(-60, "pool_const", lambda: G.memset(head_ones[:, :], 1.0))
        half_c = on_pool(-60, "pool_const", lambda: G.memset(minus_half[:, :], -0.5))
        ident_ok = on_pool(-60, "pool_const", lambda: G.affine_select(
            out=ident[:, :], in_=ident[:, :], compare_op=ALU.not_equal, fill=1.0,
            base=0, pattern=[[-1, P]], channel_multiplier=1), [zero_id])
        by_head = head_ones[:, :].rearrange("p (h d) -> p h d", d=D)
        low_ok = on_pool(-60, "pool_const", lambda: G.affine_select(
            out=by_head, in_=by_head, compare_op=ALU.is_ge, fill=0.0,
            base=0, pattern=[[-D, HEADS], [0, D]], channel_multiplier=1), [one_head])
        heads_ok = on_pool(-60, "pool_const", lambda: G.affine_select(
            out=by_head, in_=by_head, compare_op=ALU.is_ge, fill=0.0,
            base=D - 1, pattern=[[D, HEADS], [0, D]], channel_multiplier=-1), [low_ok])

        exp_mask = 0x7F800000
        scale_ok = {}

        def weight_scale(w, slot):
            parts = []
            for i, dst in enumerate((amax_part[w], amax_part2[w])):
                parts.append(on_dve(slot, "w_max", lambda i=i, dst=dst: V.tensor_reduce(
                    dst, raw[w][:, i * n_raw // 2:(i + 1) * n_raw // 2], AX.X, ALU.max,
                    apply_absolute_value=True), [load_w[w, i]]))
            row = on_dve(slot, "w_max", lambda: V.tensor_tensor(
                amax_row[w], amax_part[w], amax_part2[w], ALU.max), parts)
            every = on_pool(slot, "w_max_all", lambda: G.partition_all_reduce(
                amax_all[w], amax_row[w], P, RMAX), [row])
            slot += 1
            power = on_dve(slot, "w_scale", lambda: V.tensor_scalar(
                pow2_raw[w].bitcast(I32), amax_all[w].bitcast(I32), exp_mask, None, ALU.bitwise_and), [every])
            power = on_dve(slot, "w_scale", lambda: V.tensor_scalar(
                pow2[w], pow2_raw[w], 2.0 ** -60, 2.0 ** 60, ALU.max, ALU.min), [power])
            unscale = on_dve(slot, "w_scale", lambda: V.tensor_scalar(
                w_unscale[w], pow2[w], 2.0 ** -W_EXP, None, ALU.mult), [power])
            inverse = on_dve(slot, "w_scale", lambda: V.reciprocal(pow2_inv[w], pow2[w]), [power])
            scale_ok[w] = on_dve(slot, "w_scale", lambda: V.tensor_scalar(
                w_scale[w], pow2_inv[w], 2.0 ** W_EXP, None, ALU.mult), [inverse, unscale])

        w_hi = {"g": wg_hi, "u": wu_hi, "d": wd_hi}
        w_lo = {"g": wg_lo, "u": wu_lo, "d": wd_lo}
        split_ok = {}

        def weight_split(w, x, slot):
            cut = slice(x * FF, (x + 1) * FF)
            hi = on_act(slot, "w_hi", lambda: S.activation(
                w_hi[w][:, cut], raw[w][:, cut], ACT.Copy, scale=w_scale[w]), [scale_ok[w]])
            split_ok[w, x] = on_dve(slot + 1, "w_lo", lambda: V.scalar_tensor_tensor(
                w_lo[w][:, cut], raw[w][:, cut], w_scale[w], w_hi[w][:, cut], ALU.mult, ALU.subtract), [hi])

        weight_scale("g", -50)
        weight_scale("u", -48)
        hscale_ok = on_dve(-46, "w_scale", lambda: V.tensor_scalar(
            h_scale, w_scale["g"], 2.0 ** -H_EXP, None, ALU.mult), [scale_ok["g"]])
        gu_ok = on_dve(-46, "w_scale", lambda: V.tensor_scalar(
            gu_unscale, w_unscale["g"], w_unscale["u"], 0.5 * 2.0 ** H_EXP, ALU.mult, ALU.mult), [scale_ok["u"]])
        weight_split("g", 0, -46)
        weight_split("u", 0, -45)
        weight_scale("d", -24)
        out_scale_ok = on_dve(-22, "w_scale", lambda: V.tensor_tensor(
            out_scale, gu_unscale, w_unscale["d"], ALU.mult), [gu_ok, scale_ok["d"]])
        weight_split("d", 0, -22)
        for x in range(1, X):
            for i, w in enumerate("gud"):
                weight_split(w, x, SL * (x - 1) + i - 1)

        att_w_ok = {}
        for i, w in enumerate("qkvo"):
            t, use, bank = on_pe_misc(-12 + 2 * i, 2, "misc", lambda bank, w=w: TE.transpose(
                bank[:, 0:P], w_att[w][:, :], ident[:, :]), [load_att[w], ident_ok])
            att_w_ok[w] = on_act(use.end, "w_att_T", lambda bank=bank, w=w: S.activation(
                w_att_T[w][:, :], bank[:, 0:P], ACT.Copy), [t])
            use.readers = [att_w_ok[w]]

        x_ok = {blk: [load_x[blk]] for blk in range(NB)}
        x_read = {blk: [] for blk in range(NB)}

        def layer_norm(blk, slot, gap=1):
            use = ln_ring.take(slot, 12)
            i, slot = use.index, use.start
            tiles = [x_tok[:, blk * TT + t, :] for t in range(TT)]

            def do_stats():
                for t in range(TT):
                    last = V.bn_stats(stats[:, i, t, :], tiles[t])
                return last

            def do_aggr():
                for t in range(TT):
                    last = V.bn_aggr(mean_var[:, i, t, :], stats[:, i, t, :])
                return last

            st = on_dve(slot, "ln_stats", do_stats, x_ok[blk] + use_free(ln_ring, use))
            ag = on_dve(slot + 1, "ln_mean_var", do_aggr, [st])
            ve = on_pool(slot + 1, "ln_var_eps", lambda: G.tensor_scalar(
                var_eps[:, i, :], mean_var[:, i, :, 1], LN_EPS, None, ALU.add), [ag])
            rs = on_pool(slot + 1, "ln_rstd", lambda: G.tensor_tensor(
                rstd[:, i, :], var_eps[:, i, :], minus_half[:, :], ALU.pow), [ve, half_c])

            def do_norm():
                for t in range(TT):
                    last = G.tensor_scalar(xn_tok[:, i, t * P:(t + 1) * P], tiles[t], mean_var[:, i, t, 0:1],
                                           rstd[:, i, t:t + 1], ALU.subtract, ALU.mult)
                return last

            nm = on_pool(slot + 2, "ln_norm", do_norm, [rs])

            def do_T(bank):
                for t in range(TT):
                    last = TE.transpose(bank[:, t * P:(t + 1) * P], xn_tok[:, i, t * P:(t + 1) * P], ident[:, :])
                return last

            tr, muse, bank = on_pe_misc(slot + 4, 1 + gap, "misc", do_T, [nm, ident_ok])
            assert muse.start <= use.end, "the layer norm's buffers are held too shortly"
            use.end = muse.start
            use.readers = [tr]
            x_read[blk] = [nm, st]
            return tr, muse, bank

        pending = []

        def use_free(ring, use):
            marker = ("free", use)
            pending.append(marker)
            return [marker]

        xn_use, xn_ready = {}, {}
        g_done, u_done, silu_done, h_done, hi_done, lo_done, d_done = {}, {}, {}, {}, {}, {}, {}
        evac_done = {}

        def prepare(s, slot):
            tr, muse, bank = layer_norm(segs[s][1], slot, gap=2)
            use = xn_ring.take(muse.start, NC * (s + 1) - muse.start, fixed=True)
            xn_use[s], i = use, use.index
            hi = on_act(muse.start + 1, "xn_hi", lambda: S.activation(
                xn_hi[:, i, :], bank[:, :], ACT.Copy), [tr] + use_free(xn_ring, use))
            lo = on_dve(muse.start + 2, "xn_lo", lambda: V.tensor_tensor(
                xn_lo[:, i, :], bank[:, :], xn_hi[:, i, :], ALU.subtract), [hi])
            muse.readers = [lo]
            xn_ready[s] = [lo]

        def ffn_products(n):
            s, c = divmod(n, NC)
            i = xn_use[s].index
            cut = slice(c * P, (c + 1) * P)
            hi, lo = xn_hi[:, i, :], xn_lo[:, i, :]

            def three(bank, w_hi, w_lo):
                TE.matmul(bank[:, :], w_hi[:, cut], hi, start=True, stop=False)
                TE.matmul(bank[:, :], w_hi[:, cut], lo, start=False, stop=False)
                return TE.matmul(bank[:, :], w_lo[:, cut], hi, start=False, stop=True)

            first = s == 0 and c % SL == 0
            g_done[n] = on_pe(n, "gate", lambda: three(gate_ps[n % 2], wg_hi, wg_lo),
                              (xn_ready[s] if c == 0 else []) + ([split_ok["g", c // SL]] if first else [])
                              + [silu_done.get(n - 2)])
            u_done[n] = on_pe(n, "up", lambda: three(up_ps[n % 2], wu_hi, wu_lo),
                              ([split_ok["u", c // SL]] if first else []) + [h_done.get(n - 2)])
            if c == NC - 1:
                xn_use[s].readers = [u_done[n]]

        def ffn_down(n):
            s, c = divmod(n, NC)
            cut, i, bank = slice(c * P, (c + 1) * P), n % NH, down_ps[s % 2]

            def three():
                TE.matmul(bank[:, :], wd_hi[:, cut], h_hi[:, i, :], start=c == 0, stop=False)
                TE.matmul(bank[:, :], wd_lo[:, cut], h_hi[:, i, :], start=False, stop=False)
                return TE.matmul(bank[:, :], wd_hi[:, cut], h_lo[:, i, :], start=False, stop=c == NC - 1)

            d_done[n] = on_pe(n + LAG, "down", three,
                              [lo_done[n], evac_done.get(s - 2) if c == 0 else None]
                              + ([split_ok["d", c // SL]] if s == 0 and c % SL == 0 else []))

        def ffn_silu(n):
            silu_done[n] = on_act(n, "silu", lambda: S.activation(
                silu_sb[:, n % 3, :], gate_ps[n % 2][:, :], ACT.Silu, scale=w_unscale["g"]),
                [g_done[n], h_done.get(n - 3)] + ([scale_ok["g"]] if n == 0 else []))

        def ffn_h(n):
            h_done[n] = on_dve(n, "h", lambda: V.scalar_tensor_tensor(
                h_sb[:, n % 3, :], silu_sb[:, n % 3, :], h_scale, up_ps[n % 2][:, :], ALU.mult, ALU.mult),
                [silu_done[n], u_done[n], lo_done.get(n - 3)] + ([hscale_ok] if n == 0 else []))

        def ffn_hi(n):
            hi_done[n] = on_act(n + 1, "h_hi", lambda: S.activation(
                h_hi[:, n % NH, :], h_sb[:, n % 3, :], ACT.Copy), [h_done[n], d_done.get(n - NH)])

        def ffn_lo(n):
            lo_done[n] = on_dve(n + 1, "h_lo", lambda: V.tensor_tensor(
                h_lo[:, n % NH, :], h_sb[:, n % 3, :], h_hi[:, n % NH, :], ALU.subtract),
                [hi_done[n], d_done.get(n - NH)])

        resid_T, resid_done = {}, {}

        def finish_segment(s):
            f, blk = segs[s]
            end = NC * (s + 1) - 1 + LAG
            evac_done[s] = on_act(end + 1, "down_evac", lambda: S.activation(
                down_sb[:, s % 2, :], down_ps[s % 2][:, :], ACT.Copy, scale=out_scale),
                [d_done[NC * (s + 1) - 1], resid_T.get(s - 2)] + ([out_scale_ok] if s == 0 else []))

            def do_T(bank):
                for t in range(TT):
                    last = TE.transpose(bank[:, t * P:(t + 1) * P], down_sb[:, s % 2, t * P:(t + 1) * P], ident[:, :])
                return last

            tr, muse, bank = on_pe_misc(end + 2, 2, "misc", do_T, [evac_done[s], ident_ok])
            resid_T[s] = tr
            xb = x_tok[:, blk * TT:(blk + 1) * TT, :].rearrange("p t e -> p (t e)")
            add = on_dve(muse.start + 1, "resid", lambda: V.tensor_tensor(xb, bank[:, :], xb, ALU.add),
                         [tr] + x_ok[blk] + x_read[blk])
            muse.readers = [add]
            x_ok[blk], resid_done[s] = [add], add
            if f == 2:
                dma(muse.start + 2, "out", block_rows(out_rows, blk), x_tok[:, blk * TT:(blk + 1) * TT, :], [add])
            return muse.start + 2

        last = {}

        def attention(b, slot):
            ka, kl, qa, ql = part["k_act"], part["k_lin"], part["q_act"], part["q_lin"]
            vT, rden, num = part["v_T"], part["rden"], part["num"]
            act_of = {"k": (ka, kl), "q": (qa, ql)}
            raw_ok = {"k": [], "q": []}
            v_ok = []
            for j in range(BB):
                blk = b * BB + j
                half = slice(j * T, (j + 1) * T)
                tr, muse, bank = layer_norm(blk, slot)
                xn = on_act(muse.start + 1, "att_xn", lambda bank=bank: S.activation(
                    xn_T[:, :], bank[:, :], ACT.Copy), [tr] + last.get("xn_T", []))
                muse.readers = [xn]
                xb = x_tok[:, blk * TT:(blk + 1) * TT, :]
                bias = bo_all[:, :].rearrange("p (a e) -> p a e", a=1).to_broadcast([P, TT, E])
                x_ok[blk] = [on_pool(muse.start + 1, "x_bias", lambda xb=xb, bias=bias: G.tensor_tensor(
                    xb, xb, bias, ALU.add), x_ok[blk] + x_read[blk] + [load_bo])]
                x_read[blk] = []
                at = muse.start + 2
                for w in "kqv":
                    pr, use, bank = on_pe_misc(at, 2, "misc", lambda bank, w=w: TE.matmul(
                        bank[:, :], w_att_T[w][:, :], xn_T[:, :], start=True, stop=True), [xn, att_w_ok[w]])
                    at = use.start + 1
                    if w == "v":
                        ev = on_act(use.start + 1, "v_evac", lambda bank=bank, half=half: S.activation(
                            vT[:, half], bank[:, :], ACT.Copy), [pr] + last.get("v_T", []))
                        v_ok.append(ev)
                    else:
                        act, lin = act_of[w]
                        on_act(use.start + 1, f"{w}_evac", lambda bank=bank, act=act, half=half: S.activation(
                            act[:, half], bank[:, :], ACT.Copy), [pr] + last.get(w + "_act", []))
                        ev = on_act(use.start + 1, f"{w}_evac", lambda bank=bank, lin=lin, half=half: S.activation(
                            lin[:, half], bank[:, :], ACT.Relu), [pr] + last.get(w + "_lin", []))
                        raw_ok[w].append(ev)
                    use.readers = [ev]
                last["xn_T"] = [pr]
                slot += 6
            at += 2
            phi_ok = {}
            for w in "kq":
                act, lin = act_of[w]
                ex = on_act(at, "exp", lambda act=act: S.activation(act[:, :], act[:, :], ACT.Exp), raw_ok[w])
                phi_ok[w] = [on_dve(at + 1 + j + (2 if w == "q" else 0), "phi",
                                    lambda act=act, lin=lin, j=j: V.scalar_tensor_tensor(
                    act[:, j * T:(j + 1) * T], act[:, j * T:(j + 1) * T], 1.0, lin[:, j * T:(j + 1) * T],
                    ALU.min, ALU.add), [ex]) for j in range(BB)]
            store = {w: dma(at + 3 + 2 * i, f"store_{w}", scratch[b, i, :, :], act_of[w][0][:, :], phi_ok[w])
                     for i, w in enumerate("kq")}
            at += 7
            rep = {}
            pace = 4 * BB
            for d in range(D):
                for i, w in enumerate("kq"):
                    start = at - 2 + d * pace - pace if d else at - 2
                    use = rep_ring[w].take(start, at + (d + 1) * pace + 4 - start, fixed=True)
                    buf = part[w + "_rep"][:, use.index * L:(use.index + 1) * L]
                    src = scratch[b, i, :, :].rearrange("(h d) t -> h d t", d=D)[:, d:d + 1, :]
                    ld = dma(use.start, f"{w}_rep{use.index}", buf, src.to_broadcast([HEADS, D, L]),
                             [store[w]] + use_free(rep_ring[w], use))
                    rep[w, d] = use, buf, ld
            z = None
            pz = []
            for j in range(BB):
                half = slice(j * T, (j + 1) * T)
                z0 = z
                z = on_dve(at - 1 + j, "z_scan", lambda half=half, j=j: V.tensor_tensor_scan(
                    kl[:, half], ka[:, half], ka[:, half], 0.0 if j == 0 else kl[:, j * T - 1:j * T],
                    ALU.add, ALU.bypass), phi_ok["k"] + [z0])
                pz.append(on_pool(at + j, "q_z", lambda half=half: G.tensor_tensor(
                    ql[:, half], qa[:, half], kl[:, half], ALU.mult), [z] + phi_ok["q"]))
            rden_ok = [None, None]
            recips = []
            for j in range(BB):
                half = slice(j * T, (j + 1) * T)
                dn, use, bank = on_pe_misc(at + 2 + j, 2, "misc", lambda bank, half=half: TE.matmul(
                    bank[:, :], head_ones[:, :], ql[:, half], start=True, stop=True), [pz[j], heads_ok])
                dn_sb = on_act(use.start + 1, "den_evac", lambda bank=bank, half=half: S.activation(
                    rden[:, half], bank[:, :], ACT.Copy, bias=ATT_EPS), [dn] + last.get("rden", []))
                use.readers = [dn_sb]
                for i in range(TT):
                    cut = slice(j * T + i * P, j * T + (i + 1) * P)
                    recips.append(on_dve(at + 6 + pace // 2 * (j * TT + i), "recip", lambda cut=cut: V.reciprocal(
                        rden[:, cut], rden[:, cut]), [dn_sb]))
                rden_ok[j] = recips[-1]
            last["k_lin"], last["q_lin"] = pz, [dn]
            last["k_act"], last["q_act"] = [store["k"], z], [store["q"]] + pz
            num_ok = [None] * BB
            carry = {}
            for i in range(D * BB):
                d, j = divmod(i, BB)
                half = slice(j * T, (j + 1) * T)
                ku, kbuf, kld = rep["k", d]
                qu, qbuf, qld = rep["q", d]
                t0 = at + 4 * i
                kv = part["kv"][:, (i % 2) * T:(i % 2 + 1) * T]
                stt = part["state"][:, (i % 3) * T:(i % 3 + 1) * T]
                qs = part["qs"][:, (i % 3) * T:(i % 3 + 1) * T]
                k1 = on_pool(t0, "k_v", lambda kv=kv, kbuf=kbuf, half=half: G.tensor_tensor(
                    kv, kbuf[:, half], vT[:, half], ALU.mult), [kld, v_ok[j]] + last.get(("kv", i % 2), []))
                ku.readers = [k1]
                start_at = 0.0 if j == 0 else carry["buf"][:, T - 1:T]
                sc = on_dve(t0 + 2, "kv_scan", lambda kv=kv, stt=stt, start_at=start_at: V.tensor_tensor_scan(
                    stt, kv, kv, start_at, ALU.add, ALU.bypass),
                    [k1, carry.get("step")] + last.get(("state", i % 3), []))
                last["kv", i % 2] = [sc]
                carry = {"buf": stt, "step": sc} if j < BB - 1 else {}
                dst = num[:, half] if d == 0 else qs
                wait = last.get("num", []) if d == 0 else last.get(("qs", i % 3), [])
                m = on_dve(t0 + 3, "q_state", lambda dst=dst, qbuf=qbuf, stt=stt, half=half: V.tensor_tensor(
                    dst, qbuf[:, half], stt, ALU.mult), [sc, qld] + wait)
                qu.readers = [m]
                last["state", i % 3] = [m]
                if d:
                    num_ok[j] = on_pool(t0 + 4, "num_add", lambda half=half, qs=qs: G.tensor_tensor(
                        num[:, half], num[:, half], qs, ALU.add), [m, num_ok[j]])
                    last["qs", i % 3] = [num_ok[j]]
                else:
                    num_ok[j] = m
            last["v_T"] = [k1]
            wo_read = []
            for j in range(BB):
                blk = b * BB + j
                half = slice(j * T, (j + 1) * T)
                t0 = at + 4 * (D - 1) * BB + 4 * j + 6
                dv = on_dve(t0, "att_out", lambda half=half: V.tensor_tensor(
                    num[:, half], num[:, half], rden[:, half], ALU.mult), [num_ok[j], rden_ok[j]])

                def do_wo(bank, j=j):
                    for t in range(TT):
                        mm = TE.matmul(bank[:, t * P:(t + 1) * P], num[:, j * T + t * P:j * T + (t + 1) * P],
                                       w_att_T["o"][:, :], start=True, stop=True)
                    return mm

                wo, use, bank = on_pe_misc(t0 + 1, 2, "misc", do_wo, [dv, att_w_ok["o"]])
                xb = x_tok[:, blk * TT:(blk + 1) * TT, :].rearrange("p t e -> p (t e)")
                add = on_dve(use.start + 1, "resid", lambda xb=xb, bank=bank: V.tensor_tensor(
                    xb, bank[:, :], xb, ALU.add), [wo] + x_ok[blk])
                use.readers = [add]
                x_ok[blk], x_read[blk] = [add], []
                wo_read.append(wo)
                last["rden"] = [dv]
            last["num"] = wo_read
            return use.start + 2

        att_len = 110
        first_after = {b: NC * (seg_of[1, b * BB + BB - 1] + 1) + LAG + 5 for b in range(B)}
        att_at = {B - 1: first_after[B - 1]}
        for b in range(B - 2, -1, -1):
            att_at[b] = att_at[b + 1] - att_len
            assert att_at[b] >= first_after[b] or b == 0
        att_at[0] = first_after[0]
        events = []
        for s in range(len(segs)):
            events.append((NC * s - 12 if s else -44, 1, "prepare", s))
            events.append((NC * (s + 1) + LAG, 0, "finish", s))
        events += [(att_at[b], 2, "attention", b) for b in range(B)]
        events += [(n, 3, "unit", n) for n in range(NU)]
        att_end = {}
        for slot, _, what, i in sorted(events):
            if what == "unit":
                ffn_products(i)
                ffn_silu(i)
                ffn_h(i)
                ffn_hi(i)
                ffn_lo(i)
                ffn_down(i)
            elif what == "finish":
                finish_segment(i)
            elif what == "attention":
                att_end[i] = attention(i, slot)
            else:
                if segs[i][0] == 2:
                    slot = max(slot, att_end[segs[i][1] // BB] if segs[i][1] % BB == BB - 1 else slot)
                prepare(i, slot)

        for ring in (misc, xn_ring, ln_ring, *rep_ring.values()):
            ring.link()

        core_signals = {"gate": 0, "up": 1, "down": 2, "silu": 0, "h_hi": 1, "h": 0, "h_lo": 1}
        engines = {e: [] for e in ("sync", "tensor", "scalar", "vector", "gpsimd")}
        for s in steps:
            s.after = [r for a in s.after for r in (a[1].free() if isinstance(a, tuple) else [a])]
            if s.use is not None:
                s.after += s.use.free()
            engines[s.engine].append(s)
        awaited = {id(a) for s in steps for a in s.after}
        signals = {}
        for queue in engines.values():
            queue.sort(key=lambda s: (s.slot, core_signals.get(s.sem_name, 5)))
            for s in queue:
                if id(s) in awaited or s.sem_name == "out":
                    entry = signals.setdefault(s.sem_name, [s.engine, 0])
                    assert entry[0] == s.engine, "a semaphore is signalled by one engine"
                    entry[1] += s.inc
                    s.value = entry[1]
        sems = {name: ctx.enter_context(nc.semaphore(name)) for name in signals}

        def run(engine, eng):
            seen = {}
            for s in engines[engine]:
                for a in s.after:
                    if seen.get(a.sem_name, 0) < a.value:
                        eng.wait_ge(sems[a.sem_name], a.value)
                        seen[a.sem_name] = a.value
                made = s.emit(eng)
                if s.value is not None:
                    made.then_inc(sems[s.sem_name], s.inc)

        block = ctx.enter_context(nc.Block())

        @block.sync
        def _(eng):
            run("sync", eng)
            eng.wait_ge(sems["out"], signals["out"][1])

        @block.tensor
        def _(eng):
            run("tensor", eng)

        @block.scalar
        def _(eng):
            run("scalar", eng)

        @block.vector
        def _(eng):
            run("vector", eng)

        @block.gpsimd
        def _(eng):
            run("gpsimd", eng)


_INS = ['L0_attn_x', 'L0_attn_Wq', 'L0_attn_Wk', 'L0_attn_Wv', 'L0_attn_Wo', 'L0_attn_bo',
        'L0_ffn_Wg', 'L0_ffn_Wu', 'L0_ffn_Wd']


def kernel(**inputs):
    import numpy as _np
    import concourse.bacc as _bacc
    from concourse import mybir as _mybir
    from concourse.bass_utils import run_bass_kernel_spmd as _run

    nc = _bacc.Bacc("TRN2", target_bir_lowering=False, num_devices=1)
    arrays, args = {}, []
    for name in _INS:
        a = _np.ascontiguousarray(inputs[name])
        arrays[f"in_{name}"] = a
        args.append(nc.dram_tensor(f"in_{name}", a.shape, _mybir.dt.from_np(a.dtype), kind="ExternalInput").ap())
    shape = inputs['L0_attn_x'].shape
    out = nc.dram_tensor("out_0", shape, _mybir.dt.float32, kind="ExternalOutput").ap()
    macaron_program(nc, *args, out)
    r = _run(nc, [arrays], core_ids=[0])
    return r.results[0]["out_0"]
```

```python
from contextlib import ExitStack

import concourse.bass as bass
from concourse import mybir

P = 128
F32 = mybir.dt.float32
F16 = mybir.dt.float16
I32 = mybir.dt.int32
ALU = mybir.AluOpType
ACT = mybir.ActivationFunctionType
AX = mybir.AxisListType
RMAX = bass.bass_isa.ReduceOp.max

LN_EPS = 1e-5
ATT_EPS = 1e-5
HEADS = 16
W_EXP = 4
H_EXP = 2 * (7 + W_EXP + 1) - 15
LAG = 3


class Step:

    def __init__(self, engine, slot, signal, emit, after, inc=1):
        self.engine, self.slot, self.sem_name, self.emit = engine, slot, signal, emit
        self.use, self.value = None, None
        self.after, self.inc = [s for s in after if s is not None], inc


class Use:

    def __init__(self, start, end, index):
        self.start, self.end, self.index = start, end, index
        self.readers, self.before = [], None

    def free(self):
        return self.before.readers if self.before else []


class Ring:

    def __init__(self, n):
        self.uses = [[] for _ in range(n)]

    def take(self, start, length, fixed=False):
        while True:
            for index, uses in enumerate(self.uses):
                if all(u.end < start or u.start > start + length - 1 for u in uses):
                    use = Use(start, start + length - 1, index)
                    uses.append(use)
                    return use
            assert not fixed, "no buffer is free"
            start += 1

    def free_from(self, start, length):
        while any(u.end >= start and u.start < start + length for uses in self.uses for u in uses):
            start += 1
        return start

    def link(self):
        for uses in self.uses:
            uses.sort(key=lambda u: u.start)
            for a, b in zip(uses, uses[1:]):
                b.before = a


def macaron_program(nc, x_d, wq_d, wk_d, wv_d, wo_d, bo_d, wg_d, wu_d, wd_d, out_d):
    B, L, E = x_d.shape
    X, _, FF = wg_d.shape
    D = E // HEADS
    T = 512
    TT = T // P
    BB = L // T
    NB = B * BB
    SL = FF // P
    NC = X * SL
    assert E == P and BB == 2 and FF % P == 0 and L % T == 0

    order = [(1, 0), (1, 1), (1, 2)]
    for b in range(3, B):
        order += [(2, b - 3), (1, b)]
    order += [(2, b) for b in range(B - 3, B)]
    segs = [(f, b * BB + j) for f, b in order for j in range(BB)]
    seg_of = {fb: s for s, fb in enumerate(segs)}
    NU = len(segs) * NC

    ctx = ExitStack()
    with ctx:
        def sb(name, shape, dt=F32):
            return ctx.enter_context(nc.sbuf_tensor(name, shape, dt))

        wg_hi, wg_lo = sb("wg_hi", [P, NC * P], F16), sb("wg_lo", [P, NC * P], F16)
        wu_hi, wu_lo = sb("wu_hi", [P, NC * P], F16), sb("wu_lo", [P, NC * P], F16)
        wd_hi, wd_lo = sb("wd_hi", [P, NC * P], F16), sb("wd_lo", [P, NC * P], F16)
        x_tok = sb("x_tok", [P, NB * TT, E])
        n_raw = NC * P
        names = [("k_act", L), ("k_lin", L), ("q_act", L), ("q_lin", L), ("v_T", L), ("rden", L), ("num", L),
                 ("k_rep", 3 * L), ("q_rep", 3 * L), ("kv", 2 * T), ("state", 3 * T), ("qs", 3 * T)]
        arena = sb("arena", [P, max(3 * n_raw, sum(n for _, n in names))])
        raw = {w: arena[:, i * n_raw:(i + 1) * n_raw] for i, w in enumerate(("g", "u", "d"))}
        part, at = {}, 0
        for name, n in names:
            part[name] = arena[:, at:at + n]
            at += n
        silu_sb = sb("silu_sb", [P, 3, T])
        h_sb = sb("h_sb", [P, 3, T])
        NH = 5
        h_hi, h_lo = sb("h_hi", [P, NH, T], F16), sb("h_lo", [P, NH, T], F16)
        NX, NL = 3, 3
        xn_hi, xn_lo = sb("xn_hi", [P, NX, T], F16), sb("xn_lo", [P, NX, T], F16)
        down_sb = sb("down_sb", [P, 2, T])
        xn_tok = sb("xn_tok", [P, NL, T])
        xa_hi, xa_lo = sb("xa_hi", [P, BB, T], F16), sb("xa_lo", [P, BB, T], F16)
        stats = sb("stats", [P, NL, TT, 6])
        mean_var = sb("mean_var", [P, NL, TT, 2])
        var_eps = sb("var_eps", [P, NL, TT])
        rstd = sb("rstd", [P, NL, TT])
        minus_half = sb("minus_half", [P, TT])
        ident = sb("ident", [P, P])
        head_ones = sb("head_ones", [P, P])
        w_att = {w: sb(f"w{w}_raw", [P, P]) for w in "qkvo"}
        w_att_T = {w: sb(f"w{w}_T", [P, P]) for w in "qkvo"}
        att_hi = {w: sb(f"w{w}_hi", [P, P], F16) for w in "qkv"}
        att_lo = {w: sb(f"w{w}_lo", [P, P], F16) for w in "qkv"}
        bo_all = sb("bo_all", [P, P])
        warm = sb("warm", [P, TT])
        scal = sb("scal", [P, 48])

        def col(i):
            return scal[:, i:i + 1]
        amax_part = sb("amax_part", [P, 3, 4])
        scaled = "gudqkv"
        at_w = {w: 6 * i for i, w in enumerate(scaled)}
        amax_row = {w: col(at_w[w]) for w in scaled}
        amax_all = {w: col(at_w[w] + 1) for w in scaled}
        pow2_raw = {w: col(at_w[w] + 2) for w in scaled}
        pow2 = {w: col(at_w[w] + 3) for w in scaled}
        w_scale = {w: col(at_w[w] + 4) for w in scaled}
        w_unscale = {w: col(at_w[w] + 5) for w in scaled}
        pow2_inv = {w: sb(f"w{w}_pow2_inv", [P, 1])[:, :] for w in scaled}
        h_scale, gu_unscale, out_scale = col(36), col(37), col(38)

        psum = [ctx.enter_context(nc.psum_tensor(f"bank{i}", [P, T], F32)) for i in range(8)]
        gate_ps, up_ps, down_ps, misc_ps = psum[0:2], psum[2:4], psum[4:6], psum[6:8]
        scratch = nc.dram_tensor("rep_scratch", (B, 2, P, L), F32, kind="Internal").ap()

        steps = []

        def step(engine, slot, signal, emit, after=(), inc=1):
            s = Step(engine, slot, signal, emit, after, inc)
            steps.append(s)
            return s

        misc = Ring(2)
        xn_ring, ln_ring = Ring(NX), Ring(NL)
        rep_ring = {"k": Ring(3), "q": Ring(3)}

        def dma(slot, signal, out, in_, after=()):
            return step("sync", slot, signal, lambda e: e.dma_start(out, in_), after, 16)

        V, S, G, TE = nc.vector, nc.scalar, nc.gpsimd, nc.tensor

        def on_dve(slot, signal, emit, after=()):
            return step("vector", slot, signal, lambda e: emit(), after)

        def on_act(slot, signal, emit, after=()):
            return step("scalar", slot, signal, lambda e: emit(), after)

        def on_pool(slot, signal, emit, after=()):
            return step("gpsimd", slot, signal, lambda e: emit(), after)

        def on_pe(slot, signal, emit, after=()):
            return step("tensor", slot, signal, lambda e: emit(), after)

        def on_pe_misc(slot, hold, signal, emit, after=()):
            use = misc.take(slot, hold)
            bank = misc_ps[use.index]
            s = step("tensor", use.start, signal, lambda e: emit(bank), after)
            s.use = use
            return s, use, bank

        x_rows = x_d.rearrange("b l e -> (b l) e")
        out_rows = out_d.rearrange("b l e -> (b l) e")

        def block_rows(rows, blk):
            return rows[blk * T:(blk + 1) * T, :].rearrange("(t p) e -> p t e", p=P)

        load_x = {}

        def load_block(blk, slot):
            load_x[blk] = dma(slot, f"x_in{blk}", x_tok[:, blk * TT:(blk + 1) * TT, :], block_rows(x_rows, blk))

        load_block(0, -70)
        NP = 4
        load_w = {}
        for w, src in (("g", wg_d), ("u", wu_d)):
            for i in range(NP):
                dst = raw[w][:, i * n_raw // NP:(i + 1) * n_raw // NP].rearrange("p (x f) -> p x f", f=FF)
                load_w[w, i] = dma(-59, f"w{w}_in{i}", dst,
                                   src[i * X // NP:(i + 1) * X // NP, :, :].rearrange("x e f -> e x f"))
        for i in range(NP):
            dst = raw["d"][:, i * n_raw // NP:(i + 1) * n_raw // NP].rearrange("p (c e) -> p c e", e=E)
            load_w["d", i] = dma(-58, f"wd_in{i}", dst,
                                 wd_d[i * X // NP:(i + 1) * X // NP, :, :].rearrange("x (j p) e -> p (x j) e", p=P))
        load_block(1, -57)
        load_att = {w: dma(-56, f"w{w}_in", w_att[w][:, :], src)
                    for w, src in zip("qkvo", (wq_d, wk_d, wv_d, wo_d))}
        load_bo = dma(-56, "bo_in", bo_all[:, :], bo_d.rearrange("(a e) -> a e", a=1).to_broadcast([P, E]))
        for blk in range(2, NB):
            load_block(blk, -55)

        zero_id = on_pool(-70, "pool_const", lambda: G.memset(ident[:, :], 0.0))
        one_head = on_pool(-70, "pool_const", lambda: G.memset(head_ones[:, :], 1.0))
        half_c = on_pool(-70, "pool_const", lambda: G.memset(minus_half[:, :], -0.5))
        ident_ok = on_pool(-70, "pool_const", lambda: G.affine_select(
            out=ident[:, :], in_=ident[:, :], compare_op=ALU.not_equal, fill=1.0,
            base=0, pattern=[[-1, P]], channel_multiplier=1), [zero_id])
        by_head = head_ones[:, :].rearrange("p (h d) -> p h d", d=D)
        low_ok = on_pool(-70, "pool_const", lambda: G.affine_select(
            out=by_head, in_=by_head, compare_op=ALU.is_ge, fill=0.0,
            base=0, pattern=[[-D, HEADS], [0, D]], channel_multiplier=1), [one_head])
        heads_ok = on_pool(-70, "pool_const", lambda: G.affine_select(
            out=by_head, in_=by_head, compare_op=ALU.is_ge, fill=0.0,
            base=D - 1, pattern=[[D, HEADS], [0, D]], channel_multiplier=-1), [low_ok])

        on_act(-60, "warm", lambda: S.activation(warm[:, :], minus_half[:, :], ACT.Silu), [half_c])

        exp_mask = 0x7F800000
        scale_ok = {}

        def weight_max(w, slot):
            n = "gud".index(w)
            parts = [on_dve(slot, "w_max", lambda i=i: V.tensor_reduce(
                amax_part[:, n, i:i + 1], raw[w][:, i * n_raw // NP:(i + 1) * n_raw // NP], AX.X, ALU.max,
                apply_absolute_value=True), [load_w[w, i]]) for i in range(NP)]
            return on_dve(slot, "w_max", lambda: V.tensor_reduce(
                amax_row[w], amax_part[:, n, :], AX.X, ALU.max), parts)

        def weight_scale(w, slot, row):
            every = on_pool(slot, "w_max_all", lambda: G.partition_all_reduce(
                amax_all[w], amax_row[w], P, RMAX), [row])
            slot += 1
            power = on_dve(slot, "w_scale", lambda: V.tensor_scalar(
                pow2_raw[w].bitcast(I32), amax_all[w].bitcast(I32), exp_mask, None, ALU.bitwise_and), [every])
            power = on_dve(slot, "w_scale", lambda: V.tensor_scalar(
                pow2[w], pow2_raw[w], 2.0 ** -60, 2.0 ** 60, ALU.max, ALU.min), [power])
            unscale = on_dve(slot, "w_scale", lambda: V.tensor_scalar(
                w_unscale[w], pow2[w], 2.0 ** -W_EXP, None, ALU.mult), [power])
            inverse = on_dve(slot, "w_scale", lambda: V.reciprocal(pow2_inv[w], pow2[w]), [power])
            scale_ok[w] = on_dve(slot, "w_scale", lambda: V.tensor_scalar(
                w_scale[w], pow2_inv[w], 2.0 ** W_EXP, None, ALU.mult), [inverse, unscale])

        w_hi = {"g": wg_hi, "u": wu_hi, "d": wd_hi}
        w_lo = {"g": wg_lo, "u": wu_lo, "d": wd_lo}
        split_ok = {}

        def weight_split(w, x, slot):
            cut = slice(x * FF, (x + 1) * FF)
            hi = on_act(slot, "w_hi", lambda: S.activation(
                w_hi[w][:, cut], raw[w][:, cut], ACT.Copy, scale=w_scale[w]), [scale_ok[w]])
            split_ok[w, x] = on_dve(slot + 1, "w_lo", lambda: V.scalar_tensor_tensor(
                w_lo[w][:, cut], raw[w][:, cut], w_scale[w], w_hi[w][:, cut], ALU.mult, ALU.subtract), [hi])

        weight_scale("g", -54, weight_max("g", -57))
        weight_scale("u", -50, weight_max("u", -50))
        hscale_ok = on_dve(-46, "w_scale", lambda: V.tensor_scalar(
            h_scale, w_scale["g"], 2.0 ** -H_EXP, None, ALU.mult), [scale_ok["g"]])
        gu_ok = on_dve(-46, "w_scale", lambda: V.tensor_scalar(
            gu_unscale, w_unscale["g"], w_unscale["u"], 0.5 * 2.0 ** H_EXP, ALU.mult, ALU.mult), [scale_ok["u"]])
        weight_split("g", 0, -46)
        weight_split("u", 0, -45)
        weight_scale("d", -24, weight_max("d", -24))
        out_scale_ok = on_dve(-22, "w_scale", lambda: V.tensor_tensor(
            out_scale, gu_unscale, w_unscale["d"], ALU.mult), [gu_ok, scale_ok["d"]])
        weight_split("d", 0, -22)
        for x in range(1, X):
            for i, w in enumerate("gud"):
                weight_split(w, x, SL * (x - 1) + i - 1)

        att_w_ok = {}
        for i, w in enumerate("qkvo"):
            t, use, bank = on_pe_misc(12 + 3 * i, 2, "misc", lambda bank, w=w: TE.transpose(
                bank[:, 0:P], w_att[w][:, :], ident[:, :]), [load_att[w], ident_ok])
            copied = on_act(use.start + 1, "w_att_T", lambda bank=bank, w=w: S.activation(
                w_att_T[w][:, :], bank[:, 0:P], ACT.Copy), [t])
            use.readers = [copied]
            att_w_ok[w] = copied
            if w == "o":
                continue
            at = use.start + 3
            row = on_dve(at, "w_max", lambda w=w: V.tensor_reduce(
                amax_row[w], w_att_T[w][:, :], AX.X, ALU.max, apply_absolute_value=True), [copied])
            weight_scale(w, at + 1, row)
            hi = on_act(at + 4, "w_hi", lambda w=w: S.activation(
                att_hi[w][:, :], w_att_T[w][:, :], ACT.Copy, scale=w_scale[w]), [scale_ok[w]])
            att_w_ok[w] = on_dve(at + 5, "w_lo", lambda w=w: V.scalar_tensor_tensor(
                att_lo[w][:, :], w_att_T[w][:, :], w_scale[w], att_hi[w][:, :], ALU.mult, ALU.subtract), [hi])

        x_ok = {blk: [load_x[blk]] for blk in range(NB)}
        x_read = {blk: [] for blk in range(NB)}

        def layer_norm(blk, slot, gap=1):
            use = ln_ring.take(slot, 14)
            i, slot = use.index, use.start
            tiles = [x_tok[:, blk * TT + t, :] for t in range(TT)]

            def do_stats():
                for t in range(TT):
                    last = V.bn_stats(stats[:, i, t, :], tiles[t])
                return last

            def do_aggr():
                for t in range(TT):
                    last = V.bn_aggr(mean_var[:, i, t, :], stats[:, i, t, :])
                return last

            st = on_dve(slot, "ln_stats", do_stats, x_ok[blk] + use_free(ln_ring, use))
            ag = on_dve(slot + 1, "ln_mean_var", do_aggr, [st])
            ve = on_pool(slot + 1, "ln_var_eps", lambda: G.tensor_scalar(
                var_eps[:, i, :], mean_var[:, i, :, 1], LN_EPS, None, ALU.add), [ag])
            rs = on_pool(slot + 1, "ln_rstd", lambda: G.tensor_tensor(
                rstd[:, i, :], var_eps[:, i, :], minus_half[:, :], ALU.pow), [ve, half_c])

            def do_norm():
                for t in range(TT):
                    last = G.tensor_scalar(xn_tok[:, i, t * P:(t + 1) * P], tiles[t], mean_var[:, i, t, 0:1],
                                           rstd[:, i, t:t + 1], ALU.subtract, ALU.mult)
                return last

            nm = on_pool(slot + 2, "ln_norm", do_norm, [rs])

            def do_T(bank):
                for t in range(TT):
                    last = TE.transpose(bank[:, t * P:(t + 1) * P], xn_tok[:, i, t * P:(t + 1) * P], ident[:, :])
                return last

            tr, muse, bank = on_pe_misc(slot + 6, 1 + gap, "misc", do_T, [nm, ident_ok])
            assert muse.start <= use.end, "the layer norm's buffers are held too shortly"
            use.end = muse.start
            use.readers = [tr]
            x_read[blk] = [nm, st]
            return tr, muse, bank

        pending = []

        def use_free(ring, use):
            marker = ("free", use)
            pending.append(marker)
            return [marker]

        xn_use, xn_ready = {}, {}
        g_done, u_done, silu_done, h_done, hi_done, lo_done, d_done = {}, {}, {}, {}, {}, {}, {}
        evac_done = {}

        def prepare(s, slot):
            tr, muse, bank = layer_norm(segs[s][1], slot, gap=2)
            use = xn_ring.take(muse.start, NC * (s + 1) - muse.start, fixed=True)
            xn_use[s], i = use, use.index
            hi = on_act(muse.start + 1, "xn_hi", lambda: S.activation(
                xn_hi[:, i, :], bank[:, :], ACT.Copy), [tr] + use_free(xn_ring, use))
            lo = on_dve(muse.start + 2, "xn_lo", lambda: V.tensor_tensor(
                xn_lo[:, i, :], bank[:, :], xn_hi[:, i, :], ALU.subtract), [hi])
            muse.readers = [lo]
            xn_ready[s] = [lo]

        def ffn_products(n):
            s, c = divmod(n, NC)
            i = xn_use[s].index
            cut = slice(c * P, (c + 1) * P)
            hi, lo = xn_hi[:, i, :], xn_lo[:, i, :]

            def three(bank, w_hi, w_lo):
                TE.matmul(bank[:, :], w_hi[:, cut], hi, start=True, stop=False)
                TE.matmul(bank[:, :], w_hi[:, cut], lo, start=False, stop=False)
                return TE.matmul(bank[:, :], w_lo[:, cut], hi, start=False, stop=True)

            first = s == 0 and c % SL == 0
            g_done[n] = on_pe(n, "gate", lambda: three(gate_ps[n % 2], wg_hi, wg_lo),
                              (xn_ready[s] if c == 0 else []) + ([split_ok["g", c // SL]] if first else [])
                              + [silu_done.get(n - 2)])
            u_done[n] = on_pe(n, "up", lambda: three(up_ps[n % 2], wu_hi, wu_lo),
                              ([split_ok["u", c // SL]] if first else []) + [h_done.get(n - 2)])
            if c == NC - 1:
                xn_use[s].readers = [u_done[n]]

        def ffn_down(n):
            s, c = divmod(n, NC)
            cut, i, bank = slice(c * P, (c + 1) * P), n % NH, down_ps[s % 2]

            def three():
                TE.matmul(bank[:, :], wd_hi[:, cut], h_hi[:, i, :], start=c == 0, stop=False)
                TE.matmul(bank[:, :], wd_lo[:, cut], h_hi[:, i, :], start=False, stop=False)
                return TE.matmul(bank[:, :], wd_hi[:, cut], h_lo[:, i, :], start=False, stop=c == NC - 1)

            d_done[n] = on_pe(n + LAG, "down", three,
                              [lo_done[n], evac_done.get(s - 2) if c == 0 else None]
                              + ([split_ok["d", c // SL]] if s == 0 and c % SL == 0 else []))

        def ffn_silu(n):
            silu_done[n] = on_act(n, "silu", lambda: S.activation(
                silu_sb[:, n % 3, :], gate_ps[n % 2][:, :], ACT.Silu, scale=w_unscale["g"]),
                [g_done[n], h_done.get(n - 3)] + ([scale_ok["g"]] if n == 0 else []))

        def ffn_h(n):
            h_done[n] = on_dve(n, "h", lambda: V.scalar_tensor_tensor(
                h_sb[:, n % 3, :], silu_sb[:, n % 3, :], h_scale, up_ps[n % 2][:, :], ALU.mult, ALU.mult),
                [silu_done[n], u_done[n], lo_done.get(n - 3)] + ([hscale_ok] if n == 0 else []))

        def ffn_hi(n):
            hi_done[n] = on_act(n + 1, "h_hi", lambda: S.activation(
                h_hi[:, n % NH, :], h_sb[:, n % 3, :], ACT.Copy), [h_done[n], d_done.get(n - NH)])

        def ffn_lo(n):
            lo_done[n] = on_dve(n + 1, "h_lo", lambda: V.tensor_tensor(
                h_lo[:, n % NH, :], h_sb[:, n % 3, :], h_hi[:, n % NH, :], ALU.subtract),
                [hi_done[n], d_done.get(n - NH)])

        resid_T, resid_done = {}, {}

        def finish_segment(s):
            f, blk = segs[s]
            end = NC * (s + 1) - 1 + LAG
            evac_done[s] = on_act(end + 1, "down_evac", lambda: S.activation(
                down_sb[:, s % 2, :], down_ps[s % 2][:, :], ACT.Copy, scale=out_scale),
                [d_done[NC * (s + 1) - 1], resid_T.get(s - 2)] + ([out_scale_ok] if s == 0 else []))

            def do_T(bank):
                for t in range(TT):
                    last = TE.transpose(bank[:, t * P:(t + 1) * P], down_sb[:, s % 2, t * P:(t + 1) * P], ident[:, :])
                return last

            tr, muse, bank = on_pe_misc(end + 3, 3, "misc", do_T, [evac_done[s], ident_ok])
            resid_T[s] = tr
            xb = x_tok[:, blk * TT:(blk + 1) * TT, :].rearrange("p t e -> p (t e)")
            add = on_dve(muse.start + 1, "resid", lambda: V.tensor_tensor(xb, bank[:, :], xb, ALU.add),
                         [tr] + x_ok[blk] + x_read[blk])
            muse.readers = [add]
            x_ok[blk], resid_done[s] = [add], add
            if f == 2:
                dma(muse.start + 2, "out", block_rows(out_rows, blk), x_tok[:, blk * TT:(blk + 1) * TT, :], [add])
            return muse.start + 2

        last = {}

        def project(bank, w, j):
            TE.matmul(bank[:, :], att_hi[w][:, :], xa_hi[:, j, :], start=True, stop=False)
            TE.matmul(bank[:, :], att_hi[w][:, :], xa_lo[:, j, :], start=False, stop=False)
            return TE.matmul(bank[:, :], att_lo[w][:, :], xa_hi[:, j, :], start=False, stop=True)

        def attention(b, slot):
            ka, kl, qa, ql = part["k_act"], part["k_lin"], part["q_act"], part["q_lin"]
            vT, rden, num = part["v_T"], part["rden"], part["num"]
            act_of = {"k": (ka, kl), "q": (qa, ql)}
            raw_ok = {"k": [], "q": []}
            v_ok, xn_ok = [], []
            for j in range(BB):
                blk = b * BB + j
                half = slice(j * T, (j + 1) * T)
                tr, muse, bank = layer_norm(blk, slot, gap=2)
                hi = on_act(muse.start + 1, "xa_hi", lambda bank=bank, j=j: S.activation(
                    xa_hi[:, j, :], bank[:, :], ACT.Copy), [tr] + last.get(("xa", j), []))
                xn = on_dve(muse.start + 2, "xa_lo", lambda bank=bank, j=j: V.tensor_tensor(
                    xa_lo[:, j, :], bank[:, :], xa_hi[:, j, :], ALU.subtract), [hi])
                muse.readers = [xn]
                xb = x_tok[:, blk * TT:(blk + 1) * TT, :]
                bias = bo_all[:, :].rearrange("p (a e) -> p a e", a=1).to_broadcast([P, TT, E])
                x_ok[blk] = [on_pool(muse.start + 1, "x_bias", lambda xb=xb, bias=bias: G.tensor_tensor(
                    xb, xb, bias, ALU.add), x_ok[blk] + x_read[blk] + [load_bo])]
                x_read[blk] = []
                xn_ok.append(xn)
                at = muse.start + 5
                for w in "kq":
                    pr, use, bank = on_pe_misc(at, 2, "misc", lambda bank, w=w, j=j: project(
                        bank, w, j), [xn, att_w_ok[w]])
                    at = use.start + 1
                    act, lin = act_of[w]
                    on_act(use.start + 1, f"{w}_evac", lambda w=w, bank=bank, act=act, half=half: S.activation(
                        act[:, half], bank[:, :], ACT.Copy, scale=w_unscale[w]), [pr] + last.get(w + "_act", []))
                    ev = on_act(use.start + 1, f"{w}_evac", lambda w=w, bank=bank, lin=lin, half=half: S.activation(
                        lin[:, half], bank[:, :], ACT.Relu, scale=w_unscale[w]), [pr] + last.get(w + "_lin", []))
                    raw_ok[w].append(ev)
                    use.readers = [ev]
                slot += 6
            at += 3
            v_at = misc.free_from(at + 1, BB + 1)
            at = v_at - 1
            for j in range(BB):
                half = slice(j * T, (j + 1) * T)
                pr, use, bank = on_pe_misc(v_at, 2 + j, "misc", lambda bank, j=j: project(
                    bank, "v", j), [xn_ok[j], att_w_ok["v"]])
                ev = on_act(use.end, "v_evac", lambda bank=bank, half=half: S.activation(
                    vT[:, half], bank[:, :], ACT.Copy, scale=w_unscale["v"]), [pr] + last.get("v_T", []))
                use.readers = [ev]
                v_ok.append(ev)
                last["xa", j] = [pr]
            phi_ok = {}
            for w in "kq":
                act, lin = act_of[w]
                ex = on_act(at, "exp", lambda act=act: S.activation(act[:, :], act[:, :], ACT.Exp), raw_ok[w])
                phi_ok[w] = [on_dve(at + 1 + j + (2 if w == "q" else 0), "phi",
                                    lambda act=act, lin=lin, j=j: V.scalar_tensor_tensor(
                    act[:, j * T:(j + 1) * T], act[:, j * T:(j + 1) * T], 1.0, lin[:, j * T:(j + 1) * T],
                    ALU.min, ALU.add), [ex]) for j in range(BB)]
            store = {w: dma(at + 3 + 2 * i, f"store_{w}", scratch[b, i, :, :], act_of[w][0][:, :], phi_ok[w])
                     for i, w in enumerate("kq")}
            at += 7
            rep = {}
            pace = 4 * BB
            for d in range(D):
                for i, w in enumerate("kq"):
                    start = at - 2 + d * pace - pace if d else at - 2
                    use = rep_ring[w].take(start, at + (d + 1) * pace + 4 - start, fixed=True)
                    buf = part[w + "_rep"][:, use.index * L:(use.index + 1) * L]
                    src = scratch[b, i, :, :].rearrange("(h d) t -> h d t", d=D)[:, d:d + 1, :]
                    ld = dma(use.start, f"{w}_rep{use.index}", buf, src.to_broadcast([HEADS, D, L]),
                             [store[w]] + use_free(rep_ring[w], use))
                    rep[w, d] = use, buf, ld
            z = None
            pz = []
            for j in range(BB):
                half = slice(j * T, (j + 1) * T)
                z0 = z
                z = on_dve(at - 1 + j, "z_scan", lambda half=half, j=j: V.tensor_tensor_scan(
                    kl[:, half], ka[:, half], ka[:, half], 0.0 if j == 0 else kl[:, j * T - 1:j * T],
                    ALU.add, ALU.bypass), phi_ok["k"] + [z0])
                pz.append(on_pool(at + j, "q_z", lambda half=half: G.tensor_tensor(
                    ql[:, half], qa[:, half], kl[:, half], ALU.mult), [z] + phi_ok["q"]))
            rden_ok = [None, None]
            recips = []
            for j in range(BB):
                half = slice(j * T, (j + 1) * T)
                dn, use, bank = on_pe_misc(at + 5 + j, 2, "misc", lambda bank, half=half: TE.matmul(
                    bank[:, :], head_ones[:, :], ql[:, half], start=True, stop=True), [pz[j], heads_ok])
                dn_sb = on_act(use.start + 1, "den_evac", lambda bank=bank, half=half: S.activation(
                    rden[:, half], bank[:, :], ACT.Copy, bias=ATT_EPS), [dn] + last.get("rden", []))
                use.readers = [dn_sb]
                for i in range(TT):
                    cut = slice(j * T + i * P, j * T + (i + 1) * P)
                    recips.append(on_dve(at + 9 + pace // 2 * (j * TT + i), "recip", lambda cut=cut: V.reciprocal(
                        rden[:, cut], rden[:, cut]), [dn_sb]))
                rden_ok[j] = recips[-1]
            last["k_lin"], last["q_lin"] = pz, [dn]
            last["k_act"], last["q_act"] = [store["k"], z], [store["q"]] + pz
            num_ok = [None] * BB
            carry = {}
            for i in range(D * BB):
                d, j = divmod(i, BB)
                half = slice(j * T, (j + 1) * T)
                ku, kbuf, kld = rep["k", d]
                qu, qbuf, qld = rep["q", d]
                t0 = at + 4 * i
                kv = part["kv"][:, (i % 2) * T:(i % 2 + 1) * T]
                stt = part["state"][:, (i % 3) * T:(i % 3 + 1) * T]
                qs = part["qs"][:, (i % 3) * T:(i % 3 + 1) * T]
                k1 = on_pool(t0, "k_v", lambda kv=kv, kbuf=kbuf, half=half: G.tensor_tensor(
                    kv, kbuf[:, half], vT[:, half], ALU.mult), [kld, v_ok[j]] + last.get(("kv", i % 2), []))
                ku.readers = [k1]
                start_at = 0.0 if j == 0 else carry["buf"][:, T - 1:T]
                sc = on_dve(t0 + 2, "kv_scan", lambda kv=kv, stt=stt, start_at=start_at: V.tensor_tensor_scan(
                    stt, kv, kv, start_at, ALU.add, ALU.bypass),
                    [k1, carry.get("step")] + last.get(("state", i % 3), []))
                last["kv", i % 2] = [sc]
                carry = {"buf": stt, "step": sc} if j < BB - 1 else {}
                dst = num[:, half] if d == 0 else qs
                wait = last.get("num", []) if d == 0 else last.get(("qs", i % 3), [])
                m = on_dve(t0 + 3, "q_state", lambda dst=dst, qbuf=qbuf, stt=stt, half=half: V.tensor_tensor(
                    dst, qbuf[:, half], stt, ALU.mult), [sc, qld] + wait)
                qu.readers = [m]
                last["state", i % 3] = [m]
                if d:
                    num_ok[j] = on_pool(t0 + 4, "num_add", lambda half=half, qs=qs: G.tensor_tensor(
                        num[:, half], num[:, half], qs, ALU.add), [m, num_ok[j]])
                    last["qs", i % 3] = [num_ok[j]]
                else:
                    num_ok[j] = m
            last["v_T"] = [k1]
            wo_read = []
            for j in range(BB):
                blk = b * BB + j
                half = slice(j * T, (j + 1) * T)
                t0 = at + 4 * (D - 1) * BB + 4 * j + 6
                dv = on_dve(t0, "att_out", lambda half=half: V.tensor_tensor(
                    num[:, half], num[:, half], rden[:, half], ALU.mult), [num_ok[j], rden_ok[j]])

                def do_wo(bank, j=j):
                    for t in range(TT):
                        mm = TE.matmul(bank[:, t * P:(t + 1) * P], num[:, j * T + t * P:j * T + (t + 1) * P],
                                       w_att_T["o"][:, :], start=True, stop=True)
                    return mm

                wo, use, bank = on_pe_misc(t0 + 3, 2, "misc", do_wo, [dv, att_w_ok["o"]])
                xb = x_tok[:, blk * TT:(blk + 1) * TT, :].rearrange("p t e -> p (t e)")
                add = on_dve(use.start + 1, "resid", lambda xb=xb, bank=bank: V.tensor_tensor(
                    xb, bank[:, :], xb, ALU.add), [wo] + x_ok[blk])
                use.readers = [add]
                x_ok[blk], x_read[blk] = [add], []
                wo_read.append(wo)
                last["rden"] = [dv]
            last["num"] = wo_read
            return use.start + 2

        att_len = 110
        first_after = {b: NC * (seg_of[1, b * BB + BB - 1] + 1) + LAG + 5 for b in range(B)}
        att_at = {B - 1: first_after[B - 1]}
        for b in range(B - 2, -1, -1):
            att_at[b] = att_at[b + 1] - att_len
            assert att_at[b] >= first_after[b] or b == 0
        att_at[0] = first_after[0]
        events = []
        for s in range(len(segs)):
            events.append((NC * s - 14 if s else -64, 1, "prepare", s))
            events.append((NC * (s + 1) + LAG, 0, "finish", s))
        events += [(att_at[b], 2, "attention", b) for b in range(B)]
        events += [(n, 3, "unit", n) for n in range(NU)]
        att_end = {}
        for slot, _, what, i in sorted(events):
            if what == "unit":
                ffn_products(i)
                ffn_silu(i)
                ffn_h(i)
                ffn_hi(i)
                ffn_lo(i)
                ffn_down(i)
            elif what == "finish":
                finish_segment(i)
            elif what == "attention":
                att_end[i] = attention(i, slot)
            else:
                if segs[i][0] == 2:
                    slot = max(slot, att_end[segs[i][1] // BB] if segs[i][1] % BB == BB - 1 else slot)
                prepare(i, slot)

        for ring in (misc, xn_ring, ln_ring, *rep_ring.values()):
            ring.link()

        core_signals = {"gate": 0, "up": 1, "down": 2, "silu": 0, "h_hi": 1, "h": 0, "h_lo": 1}
        engines = {e: [] for e in ("sync", "tensor", "scalar", "vector", "gpsimd")}
        for s in steps:
            s.after = [r for a in s.after for r in (a[1].free() if isinstance(a, tuple) else [a])]
            if s.use is not None:
                s.after += s.use.free()
            engines[s.engine].append(s)
        awaited = {id(a) for s in steps for a in s.after}
        signals = {}
        for queue in engines.values():
            queue.sort(key=lambda s: (s.slot, core_signals.get(s.sem_name, 5)))
            for s in queue:
                if id(s) in awaited or s.sem_name == "out":
                    entry = signals.setdefault(s.sem_name, [s.engine, 0])
                    assert entry[0] == s.engine, "a semaphore is signalled by one engine"
                    entry[1] += s.inc
                    s.value = entry[1]
        sems = {name: ctx.enter_context(nc.semaphore(name)) for name in signals}

        def run(engine, eng):
            seen = {}
            for s in engines[engine]:
                for a in s.after:
                    if seen.get(a.sem_name, 0) < a.value:
                        eng.wait_ge(sems[a.sem_name], a.value)
                        seen[a.sem_name] = a.value
                made = s.emit(eng)
                if s.value is not None:
                    made.then_inc(sems[s.sem_name], s.inc)

        block = ctx.enter_context(nc.Block())

        @block.sync
        def _(eng):
            run("sync", eng)
            eng.wait_ge(sems["out"], signals["out"][1])

        @block.tensor
        def _(eng):
            run("tensor", eng)

        @block.scalar
        def _(eng):
            run("scalar", eng)

        @block.vector
        def _(eng):
            run("vector", eng)

        @block.gpsimd
        def _(eng):
            run("gpsimd", eng)


_INS = ['L0_attn_x', 'L0_attn_Wq', 'L0_attn_Wk', 'L0_attn_Wv', 'L0_attn_Wo', 'L0_attn_bo',
        'L0_ffn_Wg', 'L0_ffn_Wu', 'L0_ffn_Wd']


def kernel(**inputs):
    import numpy as _np
    import concourse.bacc as _bacc
    from concourse import mybir as _mybir
    from concourse.bass_utils import run_bass_kernel_spmd as _run

    nc = _bacc.Bacc("TRN2", target_bir_lowering=False, num_devices=1)
    arrays, args = {}, []
    for name in _INS:
        a = _np.ascontiguousarray(inputs[name])
        arrays[f"in_{name}"] = a
        args.append(nc.dram_tensor(f"in_{name}", a.shape, _mybir.dt.from_np(a.dtype), kind="ExternalInput").ap())
    shape = inputs['L0_attn_x'].shape
    out = nc.dram_tensor("out_0", shape, _mybir.dt.float32, kind="ExternalOutput").ap()
    macaron_program(nc, *args, out)
    r = _run(nc, [arrays], core_ids=[0])
    return r.results[0]["out_0"]
```

```python
from contextlib import ExitStack

import concourse.bass as bass
from concourse import mybir

P = 128
F32 = mybir.dt.float32
F16 = mybir.dt.float16
I32 = mybir.dt.int32
ALU = mybir.AluOpType
ACT = mybir.ActivationFunctionType
AX = mybir.AxisListType

LN_EPS = 1e-5
ATT_EPS = 1e-5
HEADS = 16
W_EXP = 4
H_EXP = 2 * (7 + W_EXP + 1) - 15
LAG = 6


class Step:

    def __init__(self, engine, slot, signal, emit, after, inc=1):
        self.engine, self.slot, self.sem_name, self.emit = engine, slot, signal, emit
        self.use, self.value = None, None
        self.after, self.inc = [s for s in after if s is not None], inc


class Use:

    def __init__(self, start, end, index):
        self.start, self.end, self.index = start, end, index
        self.readers, self.before = [], None

    def free(self):
        return self.before.readers if self.before else []


class Ring:

    def __init__(self, n):
        self.uses = [[] for _ in range(n)]

    def take(self, start, length, fixed=False):
        while True:
            for index, uses in enumerate(self.uses):
                if all(u.end < start or u.start > start + length - 1 for u in uses):
                    use = Use(start, start + length - 1, index)
                    uses.append(use)
                    return use
            assert not fixed, "no buffer is free"
            start += 1

    def free_from(self, start, length):
        while any(u.end >= start and u.start < start + length for uses in self.uses for u in uses):
            start += 1
        return start

    def link(self):
        for uses in self.uses:
            uses.sort(key=lambda u: u.start)
            for a, b in zip(uses, uses[1:]):
                b.before = a


def macaron_program(nc, x_d, wq_d, wk_d, wv_d, wo_d, bo_d, wg_d, wu_d, wd_d, out_d):
    B, L, E = x_d.shape
    X, _, FF = wg_d.shape
    D = E // HEADS
    T = 512
    TT = T // P
    BB = L // T
    NB = B * BB
    SL = FF // P
    NC = X * SL
    assert E == P and BB == 2 and FF % P == 0 and L % T == 0

    order = [(1, 0), (1, 1), (1, 2)]
    for b in range(3, B):
        order += [(2, b - 3), (1, b)]
    order += [(2, b) for b in range(B - 3, B)]
    segs = [(f, b * BB + j) for f, b in order for j in range(BB)]
    seg_of = {fb: s for s, fb in enumerate(segs)}
    NU = len(segs) * NC

    ctx = ExitStack()
    with ctx:
        def sb(name, shape, dt=F32):
            return ctx.enter_context(nc.sbuf_tensor(name, shape, dt))

        wg_hi, wg_lo = sb("wg_hi", [P, NC * P], F16), sb("wg_lo", [P, NC * P], F16)
        wu_hi, wu_lo = sb("wu_hi", [P, NC * P], F16), sb("wu_lo", [P, NC * P], F16)
        wd_hi, wd_lo = sb("wd_hi", [P, NC * P], F16), sb("wd_lo", [P, NC * P], F16)
        x_tok = sb("x_tok", [P, NB * TT, E])
        n_raw = NC * P
        NKV = 3
        names = [("k_act", L), ("k_lin", L), ("q_act", L), ("q_lin", L), ("v_T", L), ("rden", L), ("num", L),
                 ("k_rep", 3 * L), ("q_rep", 3 * L), ("kv", NKV * L)]
        arena = sb("arena", [P, max(3 * n_raw, sum(n for _, n in names))])
        raw = {w: arena[:, i * n_raw:(i + 1) * n_raw] for i, w in enumerate(("g", "u", "d"))}
        part, at = {}, 0
        for name, n in names:
            part[name] = arena[:, at:at + n]
            at += n
        silu_sb = sb("silu_sb", [P, 3, T])
        NH = 2
        h_sb = sb("h_sb", [P, NH, 2, T])
        NHS = 4
        h_hi, h_lo = sb("h_hi", [P, NHS, 2, T], F16), sb("h_lo", [P, NHS, 2, T], F16)
        NX, NL = 3, 3
        xn_hi, xn_lo = sb("xn_hi", [P, NX, T], F16), sb("xn_lo", [P, NX, T], F16)
        down_sb = sb("down_sb", [P, 2, T])
        xn_tok = sb("xn_tok", [P, NL, T])
        xa_hi, xa_lo = sb("xa_hi", [P, BB, T], F16), sb("xa_lo", [P, BB, T], F16)
        stats = sb("stats", [P, NL, TT, 6])
        mean_var = sb("mean_var", [P, NL, TT, 2])
        var_eps = sb("var_eps", [P, NL, TT])
        rstd = sb("rstd", [P, NL, TT])
        minus_mean, shift = sb("minus_mean", [P, NL, TT]), sb("shift", [P, NL, TT])
        minus_half = sb("minus_half", [P, TT])
        ident = sb("ident", [P, P])
        head_ones = sb("head_ones", [P, P])
        ones, max_diag = sb("ones", [P, P]), sb("max_diag", [P, P])
        w_att = {w: sb(f"w{w}_raw", [P, P]) for w in "qkvo"}
        w_att_T = {w: sb(f"w{w}_T", [P, P]) for w in "qkvo"}
        att_hi = {w: sb(f"w{w}_hi", [P, P], F16) for w in "qkv"}
        att_lo = {w: sb(f"w{w}_lo", [P, P], F16) for w in "qkv"}
        bo_all = sb("bo_all", [P, P])
        warm = sb("warm", [P, TT])
        scal = sb("scal", [P, 48])

        def col(i):
            return scal[:, i:i + 1]
        amax_part = sb("amax_part", [P, 3, 4])
        scaled = "gudqkv"
        at_w = {w: 6 * i for i, w in enumerate(scaled)}
        amax_row = {w: col(at_w[w]) for w in scaled}
        amax_all = {w: col(at_w[w] + 1) for w in scaled}
        pow2_raw = {w: col(at_w[w] + 2) for w in scaled}
        w_scale = {w: col(at_w[w] + 4) for w in scaled}
        w_unscale = {w: col(at_w[w] + 5) for w in scaled}
        h_scale, gu_unscale, out_scale = col(36), col(37), col(38)

        psum = [ctx.enter_context(nc.psum_tensor(f"bank{i}", [P, T], F32)) for i in range(8)]
        gate_ps, up_ps, down_ps, misc_ps = psum[0:2], psum[2:4], psum[4:6], psum[6:8]
        scratch = nc.dram_tensor("rep_scratch", (B, 2, P, L), F32, kind="Internal").ap()

        steps = []

        def step(engine, slot, signal, emit, after=(), inc=1):
            s = Step(engine, slot, signal, emit, after, inc)
            steps.append(s)
            return s

        misc = Ring(2)
        xn_ring, ln_ring = Ring(NX), Ring(NL)
        rep_ring = {"k": Ring(3), "q": Ring(3)}

        def dma(slot, signal, out, in_, after=()):
            return step("sync", slot, signal, lambda e: e.dma_start(out, in_), after, 16)

        V, S, G, TE = nc.vector, nc.scalar, nc.gpsimd, nc.tensor

        def on_dve(slot, signal, emit, after=()):
            return step("vector", slot, signal, lambda e: emit(), after)

        def on_act(slot, signal, emit, after=()):
            return step("scalar", slot, signal, lambda e: emit(), after)

        def on_pool(slot, signal, emit, after=()):
            return step("gpsimd", slot, signal, lambda e: emit(), after)

        def on_pe(slot, signal, emit, after=()):
            return step("tensor", slot, signal, lambda e: emit(), after)

        def on_pe_misc(slot, hold, signal, emit, after=()):
            use = misc.take(slot, hold)
            bank = misc_ps[use.index]
            s = step("tensor", use.start, signal, lambda e: emit(bank), after)
            s.use = use
            return s, use, bank

        x_rows = x_d.rearrange("b l e -> (b l) e")
        out_rows = out_d.rearrange("b l e -> (b l) e")

        def block_rows(rows, blk):
            return rows[blk * T:(blk + 1) * T, :].rearrange("(t p) e -> p t e", p=P)

        load_x = {}

        def load_block(blk, slot):
            load_x[blk] = dma(slot, f"x_in{blk}", x_tok[:, blk * TT:(blk + 1) * TT, :], block_rows(x_rows, blk))

        load_block(0, -70)
        NP = 4
        load_w = {}
        for w, src in (("g", wg_d), ("u", wu_d)):
            for i in range(NP):
                dst = raw[w][:, i * n_raw // NP:(i + 1) * n_raw // NP].rearrange("p (x f) -> p x f", f=FF)
                load_w[w, i] = dma(-59, f"w{w}_in{i}", dst,
                                   src[i * X // NP:(i + 1) * X // NP, :, :].rearrange("x e f -> e x f"))
        for i in range(NP):
            dst = raw["d"][:, i * n_raw // NP:(i + 1) * n_raw // NP].rearrange("p (c e) -> p c e", e=E)
            load_w["d", i] = dma(-58, f"wd_in{i}", dst,
                                 wd_d[i * X // NP:(i + 1) * X // NP, :, :].rearrange("x (j p) e -> p (x j) e", p=P))
        load_block(1, -57)
        load_att = {w: dma(-56, f"w{w}_in", w_att[w][:, :], src)
                    for w, src in zip("qkvo", (wq_d, wk_d, wv_d, wo_d))}
        load_bo = dma(-56, "bo_in", bo_all[:, :], bo_d.rearrange("(a e) -> a e", a=1).to_broadcast([P, E]))
        for blk in range(2, NB):
            load_block(blk, -55)

        zero_id = on_pool(-70, "pool_const", lambda: G.memset(ident[:, :], 0.0))
        one_head = on_pool(-70, "pool_const", lambda: G.memset(head_ones[:, :], 1.0))
        ones_ok = on_pool(-70, "pool_const", lambda: G.memset(ones[:, :], 1.0))
        half_c = on_pool(-70, "pool_const", lambda: G.memset(minus_half[:, :], -0.5))
        ident_ok = on_pool(-70, "pool_const", lambda: G.affine_select(
            out=ident[:, :], in_=ident[:, :], compare_op=ALU.not_equal, fill=1.0,
            base=0, pattern=[[-1, P]], channel_multiplier=1), [zero_id])
        by_head = head_ones[:, :].rearrange("p (h d) -> p h d", d=D)
        low_ok = on_pool(-70, "pool_const", lambda: G.affine_select(
            out=by_head, in_=by_head, compare_op=ALU.is_ge, fill=0.0,
            base=0, pattern=[[-D, HEADS], [0, D]], channel_multiplier=1), [one_head])
        heads_ok = on_pool(-70, "pool_const", lambda: G.affine_select(
            out=by_head, in_=by_head, compare_op=ALU.is_ge, fill=0.0,
            base=D - 1, pattern=[[D, HEADS], [0, D]], channel_multiplier=-1), [low_ok])

        on_act(-70, "warm", lambda: S.activation(warm[:, :], minus_half[:, :], ACT.Silu), [half_c])

        early_gates = -51

        exp_mask = 0x7F800000
        scale_ok, last_spread = {}, []

        def weight_max(w, slots):
            n = "gud".index(w)
            parts = [on_dve(slot, "w_max", lambda i=i: V.tensor_reduce(
                amax_part[:, n, i:i + 1], raw[w][:, i * n_raw // NP:(i + 1) * n_raw // NP], AX.X, ALU.max,
                apply_absolute_value=True), [load_w[w, i]]) for i, slot in enumerate(slots)]
            return on_dve(slots[-1], "w_max", lambda: V.tensor_reduce(
                amax_row[w], amax_part[:, n, :], AX.X, ALU.max), parts)

        def weight_scale(w, slot, row, pe_after=0):
            diag = on_dve(slot, "w_max", lambda: V.tensor_scalar(
                max_diag[:, :], ident[:, :], amax_row[w], None, ALU.mult), [row, ident_ok] + last_spread)
            spread, use, bank = on_pe_misc(slot + pe_after, 2, "misc", lambda bank: TE.matmul(
                bank[:, 0:P], ones[:, :], max_diag[:, :], start=True, stop=True), [diag, ones_ok])
            last_spread[:] = [spread]
            slot = use.start + 1
            every = on_dve(slot, "w_scale", lambda: V.tensor_reduce(
                amax_all[w], bank[:, 0:P], AX.X, ALU.max), [spread])
            use.readers = [every]
            power = on_dve(slot, "w_scale", lambda: V.tensor_scalar(
                pow2_raw[w].bitcast(I32), amax_all[w].bitcast(I32), exp_mask, None, ALU.bitwise_and), [every])
            unscale = on_dve(slot, "w_scale", lambda: V.tensor_scalar(
                w_unscale[w], pow2_raw[w], 2.0 ** -60, 2.0 ** -W_EXP, ALU.max, ALU.mult), [power])
            scale_ok[w] = on_dve(slot, "w_scale", lambda: V.reciprocal(w_scale[w], w_unscale[w]), [unscale])

        w_hi = {"g": wg_hi, "u": wu_hi, "d": wd_hi}
        w_lo = {"g": wg_lo, "u": wu_lo, "d": wd_lo}
        split_ok = {}

        def weight_split(w, x, slot):
            cut = slice(x * FF, (x + 1) * FF)
            hi = on_act(slot, "w_hi", lambda: S.activation(
                w_hi[w][:, cut], raw[w][:, cut], ACT.Copy, scale=w_scale[w]), [scale_ok[w]])
            split_ok[w, x] = on_dve(slot + 1, "w_lo", lambda: V.scalar_tensor_tensor(
                w_lo[w][:, cut], raw[w][:, cut], w_scale[w], w_hi[w][:, cut], ALU.mult, ALU.subtract), [hi])

        weight_scale("g", -54, weight_max("g", [-57] * NP))
        weight_split("g", 0, early_gates - 1)
        weight_scale("u", -48, weight_max("u", [-54, -52, -50, -50]))
        hscale_ok = on_dve(-46, "w_scale", lambda: V.tensor_scalar(
            h_scale, w_scale["g"], 2.0 ** -H_EXP, None, ALU.mult), [scale_ok["g"]])
        gu_ok = on_dve(-46, "w_scale", lambda: V.tensor_scalar(
            gu_unscale, w_unscale["g"], w_unscale["u"], 0.5 * 2.0 ** H_EXP, ALU.mult, ALU.mult), [scale_ok["u"]])
        weight_split("u", 0, -45)
        d_diag, d_spread, d_split = -1, 0, 2
        weight_scale("d", d_diag, weight_max("d", [-48, -42, -41, -40]), d_spread - d_diag)
        out_scale_ok = on_dve(d_split, "w_scale", lambda: V.tensor_tensor(
            out_scale, gu_unscale, w_unscale["d"], ALU.mult), [gu_ok, scale_ok["d"]])
        weight_split("d", 0, d_split)
        for x in range(1, X):
            for after, w in ((-1, "g"), (0, "u"), (6, "d")):
                weight_split(w, x, SL * (x - 1) + after)

        att_w_ok = {}
        att_w_pace, spread_after = 18, 5
        for i, w in enumerate("qkvo"):
            t, use, bank = on_pe_misc(12 + att_w_pace * i, 2, "misc", lambda bank, w=w: TE.transpose(
                bank[:, 0:P], w_att[w][:, :], ident[:, :]), [load_att[w], ident_ok])
            copied = on_act(use.start + 1, "w_att_T", lambda bank=bank, w=w: S.activation(
                w_att_T[w][:, :], bank[:, 0:P], ACT.Copy), [t])
            use.readers = [copied]
            att_w_ok[w] = copied
            if w == "o":
                continue
            at = use.start + 3
            row = on_dve(at, "w_max", lambda w=w: V.tensor_reduce(
                amax_row[w], w_att_T[w][:, :], AX.X, ALU.max, apply_absolute_value=True), [copied])
            weight_scale(w, at + 1, row, spread_after)
            hi = on_act(at + spread_after + 4, "w_hi", lambda w=w: S.activation(
                att_hi[w][:, :], w_att_T[w][:, :], ACT.Copy, scale=w_scale[w]), [scale_ok[w]])
            att_w_ok[w] = on_dve(at + spread_after + 6, "w_lo", lambda w=w: V.scalar_tensor_tensor(
                att_lo[w][:, :], w_att_T[w][:, :], w_scale[w], att_hi[w][:, :], ALU.mult, ALU.subtract), [hi])

        x_ok = {blk: [load_x[blk]] for blk in range(NB)}
        x_read = {blk: [] for blk in range(NB)}

        def layer_norm(blk, slot, gap):
            use = ln_ring.take(slot, 14)
            i, slot = use.index, use.start
            tiles = [x_tok[:, blk * TT + t, :] for t in range(TT)]

            def do_stats():
                for t in range(TT):
                    last = V.bn_stats(stats[:, i, t, :], tiles[t])
                return last

            def do_aggr():
                for t in range(TT):
                    last = V.bn_aggr(mean_var[:, i, t, :], stats[:, i, t, :])
                return last

            st = on_dve(slot, "ln_stats", do_stats, x_ok[blk] + use_free(use))
            ag = on_dve(slot + 1, "ln_mean_var", do_aggr, [st])
            ve = on_pool(slot + 1, "ln_var_eps", lambda: G.tensor_scalar(
                var_eps[:, i, :], mean_var[:, i, :, 1], LN_EPS, None, ALU.add), [ag])
            rs = on_pool(slot + 1, "ln_rstd", lambda: G.tensor_tensor(
                rstd[:, i, :], var_eps[:, i, :], minus_half[:, :], ALU.pow), [ve, half_c])

            mm = on_pool(slot + 1, "ln_minus_mean", lambda: G.tensor_scalar(
                minus_mean[:, i, :], mean_var[:, i, :, 0], -1.0, None, ALU.mult), [ag])
            sh = on_pool(slot + 1, "ln_shift", lambda: G.tensor_tensor(
                shift[:, i, :], minus_mean[:, i, :], rstd[:, i, :], ALU.mult), [rs, mm])

            def do_norm(first):
                for t in (first, first + 1):
                    last = S.activation(xn_tok[:, i, t * P:(t + 1) * P], tiles[t], ACT.Identity,
                                        bias=shift[:, i, t:t + 1], scale=rstd[:, i, t:t + 1])
                return last

            for first in range(0, TT, 2):
                nm = on_act(slot + 3 + first // 2, "ln_norm", lambda first=first: do_norm(first), [sh])

            def do_T(bank):
                for t in range(TT):
                    last = TE.transpose(bank[:, t * P:(t + 1) * P], xn_tok[:, i, t * P:(t + 1) * P], ident[:, :])
                return last

            tr, muse, bank = on_pe_misc(slot + 7, 1 + gap, "misc", do_T, [nm, ident_ok])
            assert muse.start <= use.end, "the layer norm's buffers are held too shortly"
            use.end = muse.start
            use.readers = [tr]
            x_read[blk] = [nm, st]
            return tr, muse, bank

        def use_free(use):
            return [("free", use)]

        xn_use, xn_ready = {}, {}
        g_done, u_done, silu_done, h_done, hi_done, lo_done, d_done = {}, {}, {}, {}, {}, {}, {}
        evac_done = {}

        def prepare(s, slot):
            tr, muse, bank = layer_norm(segs[s][1], slot, gap=2)
            use = xn_ring.take(muse.start, NC * (s + 1) - muse.start, fixed=True)
            xn_use[s], i = use, use.index
            hi = on_act(muse.start + 1, "xn_hi", lambda: S.activation(
                xn_hi[:, i, :], bank[:, :], ACT.Copy), [tr] + use_free(use))
            lo = on_dve(muse.start + 2, "xn_lo", lambda: V.tensor_tensor(
                xn_lo[:, i, :], bank[:, :], xn_hi[:, i, :], ALU.subtract), [hi])
            muse.readers = [lo]
            xn_ready[s] = [lo]

        def ffn_products(n):
            s, c = divmod(n, NC)
            i = xn_use[s].index
            cut = slice(c * P, (c + 1) * P)
            hi, lo = xn_hi[:, i, :], xn_lo[:, i, :]

            def three(bank, w_hi, w_lo):
                TE.matmul(bank[:, :], w_hi[:, cut], hi, start=True, stop=False)
                TE.matmul(bank[:, :], w_hi[:, cut], lo, start=False, stop=False)
                return TE.matmul(bank[:, :], w_lo[:, cut], hi, start=False, stop=True)

            first = s == 0 and c % SL == 0
            g_done[n] = on_pe(n, "gate", lambda: three(gate_ps[n % 2], wg_hi, wg_lo),
                              (xn_ready[s] if c == 0 else []) + ([split_ok["g", c // SL]] if first else [])
                              + [silu_done.get(n - 2)])
            u_done[n] = on_pe(n, "up", lambda: three(up_ps[n % 2], wu_hi, wu_lo),
                              ([split_ok["u", c // SL]] if first else []) + [h_done.get(n - 2)])
            if c == NC - 1:
                xn_use[s].readers = [u_done[n]]

        def ffn_down(n):
            s, c = divmod(n, NC)
            cut, bank = slice(c * P, (c + 1) * P), down_ps[s % 2]
            i, half = n // 2 % NHS, n % 2

            def three():
                TE.matmul(bank[:, :], wd_lo[:, cut], h_hi[:, i, half, :], start=c == 0, stop=False)
                TE.matmul(bank[:, :], wd_hi[:, cut], h_hi[:, i, half, :], start=False, stop=False)
                return TE.matmul(bank[:, :], wd_hi[:, cut], h_lo[:, i, half, :], start=False, stop=c == NC - 1)

            d_done[n] = on_pe(n + LAG, "down", three,
                              [lo_done[n // 2], evac_done.get(s - 2) if c == 0 else None]
                              + ([split_ok["d", c // SL]] if s == 0 and c % SL == 0 else []))

        def ffn_silu(n):
            silu_done[n] = on_act(n, "silu", lambda: S.activation(
                silu_sb[:, n % 3, :], gate_ps[n % 2][:, :], ACT.Silu, scale=w_unscale["g"]),
                [g_done[n], h_done.get(n - 3)] + ([scale_ok["g"]] if n == 0 else []))

        def ffn_h(n):
            h_done[n] = on_dve(n, "h", lambda: V.scalar_tensor_tensor(
                h_sb[:, n // 2 % NH, n % 2, :], silu_sb[:, n % 3, :], h_scale, up_ps[n % 2][:, :],
                ALU.mult, ALU.mult),
                [silu_done[n], u_done[n], lo_done.get(n // 2 - NH)] + ([hscale_ok] if n == 0 else []))

        def ffn_split(pair):
            i, read = pair % NHS, d_done.get(2 * (pair - NHS) + 1)
            hi_done[pair] = on_act(2 * pair + 2, "h_hi", lambda: S.activation(
                h_hi[:, i, :, :], h_sb[:, pair % NH, :, :], ACT.Copy), [h_done[2 * pair + 1], read])
            lo_done[pair] = on_dve(2 * pair + 2, "h_lo", lambda: V.tensor_tensor(
                h_lo[:, i, :, :], h_sb[:, pair % NH, :, :], h_hi[:, i, :, :], ALU.subtract),
                [hi_done[pair], read])

        resid_T = {}

        def finish_segment(s):
            f, blk = segs[s]
            end = NC * (s + 1) - 1 + LAG
            evac_done[s] = on_act(end + 1, "down_evac", lambda: S.activation(
                down_sb[:, s % 2, :], down_ps[s % 2][:, :], ACT.Copy, scale=out_scale),
                [d_done[NC * (s + 1) - 1], resid_T.get(s - 2)] + ([out_scale_ok] if s == 0 else []))

            def do_T(bank):
                for t in range(TT):
                    last = TE.transpose(bank[:, t * P:(t + 1) * P], down_sb[:, s % 2, t * P:(t + 1) * P], ident[:, :])
                return last

            tr, muse, bank = on_pe_misc(end + 3, 3, "misc", do_T, [evac_done[s], ident_ok])
            resid_T[s] = tr
            xb = x_tok[:, blk * TT:(blk + 1) * TT, :].rearrange("p t e -> p (t e)")
            add = on_dve(muse.start + 1, "resid", lambda: V.tensor_tensor(xb, bank[:, :], xb, ALU.add),
                         [tr] + x_ok[blk] + x_read[blk])
            muse.readers = [add]
            x_ok[blk] = [add]
            if f == 2:
                dma(muse.start + 2, "out", block_rows(out_rows, blk), x_tok[:, blk * TT:(blk + 1) * TT, :], [add])
            return muse.start + 2

        exp_slots = []
        att_end = {}
        last = {}

        def project(bank, w, j):
            TE.matmul(bank[:, :], att_hi[w][:, :], xa_hi[:, j, :], start=True, stop=False)
            TE.matmul(bank[:, :], att_hi[w][:, :], xa_lo[:, j, :], start=False, stop=False)
            return TE.matmul(bank[:, :], att_lo[w][:, :], xa_hi[:, j, :], start=False, stop=True)

        def attention(b, slot):
            ka, kl, qa, ql = part["k_act"], part["k_lin"], part["q_act"], part["q_lin"]
            vT, rden, num = part["v_T"], part["rden"], part["num"]
            act_of = {"k": (ka, kl), "q": (qa, ql)}
            raw_ok = {"k": [], "q": []}
            v_ok, xn_ok = [], []
            for j in range(BB):
                blk = b * BB + j
                half = slice(j * T, (j + 1) * T)
                tr, muse, bank = layer_norm(blk, slot, gap=2)
                hi = on_act(muse.start + 1, "xa_hi", lambda bank=bank, j=j: S.activation(
                    xa_hi[:, j, :], bank[:, :], ACT.Copy), [tr] + last.get(("xa", j), []))
                xn = on_dve(muse.start + 2, "xa_lo", lambda bank=bank, j=j: V.tensor_tensor(
                    xa_lo[:, j, :], bank[:, :], xa_hi[:, j, :], ALU.subtract), [hi])
                muse.readers = [xn]
                xb = x_tok[:, blk * TT:(blk + 1) * TT, :]
                bias = bo_all[:, :].rearrange("p (a e) -> p a e", a=1).to_broadcast([P, TT, E])
                x_ok[blk] = [on_pool(muse.start + 1, "x_bias", lambda xb=xb, bias=bias: G.tensor_tensor(
                    xb, xb, bias, ALU.add), x_ok[blk] + x_read[blk] + [load_bo])]
                x_read[blk] = []
                xn_ok.append(xn)
                at = muse.start + 5
                for w in "kq":
                    pr, use, bank = on_pe_misc(at, 2, "misc", lambda bank, w=w, j=j: project(
                        bank, w, j), [xn, att_w_ok[w]])
                    at = use.start + 1
                    act, lin = act_of[w]
                    on_act(use.start + 1, f"{w}_evac", lambda w=w, bank=bank, act=act, half=half: S.activation(
                        act[:, half], bank[:, :], ACT.Copy, scale=w_unscale[w]), [pr] + last.get(w + "_act", []))
                    ev = on_act(use.start + 1, f"{w}_evac", lambda w=w, bank=bank, lin=lin, half=half: S.activation(
                        lin[:, half], bank[:, :], ACT.Relu, scale=w_unscale[w]), [pr] + last.get(w + "_lin", []))
                    raw_ok[w].append(ev)
                    use.readers = [ev]
                slot += 6
            at += 3
            v_at = misc.free_from(at + 1, BB + 1)
            at = v_at - 1
            for j in range(BB):
                half = slice(j * T, (j + 1) * T)
                pr, use, bank = on_pe_misc(v_at, 2 + j, "misc", lambda bank, j=j: project(
                    bank, "v", j), [xn_ok[j], att_w_ok["v"]])
                ev = on_act(use.end, "v_evac", lambda bank=bank, half=half: S.activation(
                    vT[:, half], bank[:, :], ACT.Copy, scale=w_unscale["v"]), [pr] + last.get("v_T", []))
                use.readers = [ev]
                v_ok.append(ev)
                last["xa", j] = [pr]
            phi_ok = {}
            exp_slots.append(at)
            for w in "kq":
                act, lin = act_of[w]
                ex = on_act(at, "exp", lambda act=act: S.activation(act[:, :], act[:, :], ACT.Exp), raw_ok[w])
                phi_ok[w] = [on_dve(at + 1 + j + (2 if w == "q" else 0), "phi",
                                    lambda act=act, lin=lin, j=j: V.scalar_tensor_tensor(
                    act[:, j * T:(j + 1) * T], act[:, j * T:(j + 1) * T], 1.0, lin[:, j * T:(j + 1) * T],
                    ALU.min, ALU.add), [ex]) for j in range(BB)]
            store = {w: dma(at + 3 + 2 * i, f"store_{w}", scratch[b, i, :, :], act_of[w][0][:, :], phi_ok[w])
                     for i, w in enumerate("kq")}
            at += 7 + at % 2
            rep = {}
            pace = 8
            for d in range(D):
                for i, w in enumerate("kq"):
                    start = at - 2 + d * pace - pace if d else at - 2
                    use = rep_ring[w].take(start, at + (d + 1) * pace + 4 - start, fixed=True)
                    buf = part[w + "_rep"][:, use.index * L:(use.index + 1) * L]
                    src = scratch[b, i, :, :].rearrange("(h d) t -> h d t", d=D)[:, d:d + 1, :]
                    ld = dma(use.start, f"{w}_rep{use.index}", buf, src.to_broadcast([HEADS, D, L]),
                             [store[w]] + use_free(use))
                    rep[w, d] = use, buf, ld
            z = None
            pz = []
            for j in range(BB):
                half = slice(j * T, (j + 1) * T)
                z0 = z
                z = on_dve(at - 1 + j, "z_scan", lambda half=half, j=j: V.tensor_tensor_scan(
                    kl[:, half], ka[:, half], ka[:, half], 0.0 if j == 0 else kl[:, j * T - 1:j * T],
                    ALU.add, ALU.bypass), phi_ok["k"] + [z0])
                pz.append(on_pool(at + j, "q_z", lambda half=half: G.tensor_tensor(
                    ql[:, half], qa[:, half], kl[:, half], ALU.mult), [z] + phi_ok["q"]))
            rden_ok = [None, None]
            recips = []
            for j in range(BB):
                half = slice(j * T, (j + 1) * T)
                dn, use, bank = on_pe_misc(at + 5 + j, 2, "misc", lambda bank, half=half: TE.matmul(
                    bank[:, :], head_ones[:, :], ql[:, half], start=True, stop=True), [pz[j], heads_ok])
                dn_sb = on_act(use.start + 1, "den_evac", lambda bank=bank, half=half: S.activation(
                    rden[:, half], bank[:, :], ACT.Copy, bias=ATT_EPS), [dn] + last.get("rden", []))
                use.readers = [dn_sb]
                for i in range(TT):
                    cut = slice(j * T + i * P, j * T + (i + 1) * P)
                    recips.append(on_dve(at + 7 + pace * (j * TT + i), "recip", lambda cut=cut: V.reciprocal(
                        rden[:, cut], rden[:, cut]), [dn_sb]))
                rden_ok[j] = recips[-1]
            last["k_lin"], last["q_lin"] = pz, [dn]
            last["k_act"], last["q_act"] = [store["k"], z], [store["q"]] + pz
            num_ok = [None] * BB
            for d in range(D):
                ku, kbuf, kld = rep["k", d]
                qu, qbuf, qld = rep["q", d]
                t0, buf = at + pace * d, part["kv"][:, d % NKV * L:(d % NKV + 1) * L]
                for j in range(BB):
                    half = slice(j * T, (j + 1) * T)
                    k1 = on_pool(t0 + j, "k_v", lambda buf=buf, kbuf=kbuf, half=half: G.tensor_tensor(
                        buf[:, half], kbuf[:, half], vT[:, half], ALU.mult),
                        [kld, v_ok[j]] + last.get(("kv", d % NKV), []))
                ku.readers = [k1]
                sc = on_dve(t0 + 3, "kv_scan", lambda buf=buf: V.tensor_tensor_scan(
                    buf, buf, buf, 0.0, ALU.add, ALU.bypass), [k1])
                dst = num if d == 0 else buf
                m = on_dve(t0 + 5, "q_state", lambda dst=dst, qbuf=qbuf, buf=buf: V.tensor_tensor(
                    dst, qbuf, buf, ALU.mult), [sc, qld] + (last.get("num", []) if d == 0 else []))
                qu.readers = [m]
                last["kv", d % NKV] = [m]
                for j in range(BB):
                    half = slice(j * T, (j + 1) * T)
                    if d == 0:
                        num_ok[j] = m
                        continue
                    num_ok[j] = on_pool(t0 + 6 + j, "num_add", lambda half=half, buf=buf: G.tensor_tensor(
                        num[:, half], num[:, half], buf[:, half], ALU.add), [m, num_ok[j]])
                    last["kv", d % NKV] = [num_ok[j]]
            last["v_T"] = [k1]
            wo_read = []
            for j in range(BB):
                blk = b * BB + j
                half = slice(j * T, (j + 1) * T)
                t0 = at + pace * D + 1 + 2 * j
                dv = on_dve(t0, "att_out", lambda half=half: V.tensor_tensor(
                    num[:, half], num[:, half], rden[:, half], ALU.mult), [num_ok[j], rden_ok[j]])

                def do_wo(bank, j=j):
                    for t in range(TT):
                        mm = TE.matmul(bank[:, t * P:(t + 1) * P], num[:, j * T + t * P:j * T + (t + 1) * P],
                                       w_att_T["o"][:, :], start=True, stop=True)
                    return mm

                wo, use, bank = on_pe_misc(t0 + 4, 2, "misc", do_wo, [dv, att_w_ok["o"]])
                xb = x_tok[:, blk * TT:(blk + 1) * TT, :].rearrange("p t e -> p (t e)")
                add = on_dve(use.start + 1, "resid", lambda xb=xb, bank=bank: V.tensor_tensor(
                    xb, bank[:, :], xb, ALU.add), [wo] + x_ok[blk])
                use.readers = [add]
                x_ok[blk], x_read[blk] = [add], []
                wo_read.append(wo)
                att_end[blk] = use.start + 2
                last["rden"] = [dv]
            last["num"] = wo_read

        att_len = 110
        first_after = {b: NC * (seg_of[1, b * BB + BB - 1] + 1) + LAG + 5 for b in range(B)}
        att_at = {B - 1: first_after[B - 1]}
        for b in range(B - 2, -1, -1):
            att_at[b] = att_at[b + 1] - att_len
            assert att_at[b] >= first_after[b] or b == 0
        att_at[0] = first_after[0]
        events = []
        for s in range(len(segs)):
            events.append((NC * s - 16 if s else -66, 1, "prepare", s))
            events.append((NC * (s + 1) + LAG, 0, "finish", s))
        events += [(att_at[b], 2, "attention", b) for b in range(B)]
        events += [(n, 3, "unit", n) for n in range(NU)]
        for slot, _, what, i in sorted(events):
            if what == "unit":
                ffn_products(i)
                ffn_silu(i)
                ffn_h(i)
                if i % 2:
                    ffn_split(i // 2)
                    ffn_down(i - 1)
                    ffn_down(i)
            elif what == "finish":
                finish_segment(i)
            elif what == "attention":
                attention(i, slot)
            else:
                if segs[i][0] == 2:
                    slot = max(slot, att_end[segs[i][1]])
                prepare(i, slot)

        for n in range(2):
            g_done[n].slot = early_gates
        for slot in exp_slots:
            d_done[slot + 4 - LAG].slot = slot + 3

        for ring in (misc, xn_ring, ln_ring, *rep_ring.values()):
            ring.link()

        core_signals = {"gate": 0, "up": 1, "down": 2, "silu": 0, "h_hi": 1, "h": 0, "h_lo": 1}
        engines = {e: [] for e in ("sync", "tensor", "scalar", "vector", "gpsimd")}
        for s in steps:
            s.after = [r for a in s.after for r in (a[1].free() if isinstance(a, tuple) else [a])]
            if s.use is not None:
                s.after += s.use.free()
            engines[s.engine].append(s)
        awaited = {id(a) for s in steps for a in s.after}
        signals = {}
        for queue in engines.values():
            queue.sort(key=lambda s: (s.slot, core_signals.get(s.sem_name, 5)))
            for s in queue:
                if id(s) in awaited or s.sem_name == "out":
                    entry = signals.setdefault(s.sem_name, [s.engine, 0])
                    assert entry[0] == s.engine, "a semaphore is signalled by one engine"
                    entry[1] += s.inc
                    s.value = entry[1]
        sems = {name: ctx.enter_context(nc.semaphore(name)) for name in signals}

        def run(engine, eng):
            seen = {}
            for s in engines[engine]:
                for a in s.after:
                    if seen.get(a.sem_name, 0) < a.value:
                        eng.wait_ge(sems[a.sem_name], a.value)
                        seen[a.sem_name] = a.value
                made = s.emit(eng)
                if s.value is not None:
                    made.then_inc(sems[s.sem_name], s.inc)

        block = ctx.enter_context(nc.Block())

        @block.sync
        def _(eng):
            run("sync", eng)
            eng.wait_ge(sems["out"], signals["out"][1])

        @block.tensor
        def _(eng):
            run("tensor", eng)

        @block.scalar
        def _(eng):
            run("scalar", eng)

        @block.vector
        def _(eng):
            run("vector", eng)

        @block.gpsimd
        def _(eng):
            run("gpsimd", eng)


_INS = ['L0_attn_x', 'L0_attn_Wq', 'L0_attn_Wk', 'L0_attn_Wv', 'L0_attn_Wo', 'L0_attn_bo',
        'L0_ffn_Wg', 'L0_ffn_Wu', 'L0_ffn_Wd']


def kernel(**inputs):
    import numpy as _np
    import concourse.bacc as _bacc
    from concourse import mybir as _mybir
    from concourse.bass_utils import run_bass_kernel_spmd as _run

    nc = _bacc.Bacc("TRN2", target_bir_lowering=False, num_devices=1)
    arrays, args = {}, []
    for name in _INS:
        a = _np.ascontiguousarray(inputs[name])
        arrays[f"in_{name}"] = a
        args.append(nc.dram_tensor(f"in_{name}", a.shape, _mybir.dt.from_np(a.dtype), kind="ExternalInput").ap())
    shape = inputs['L0_attn_x'].shape
    out = nc.dram_tensor("out_0", shape, _mybir.dt.float32, kind="ExternalOutput").ap()
    macaron_program(nc, *args, out)
    r = _run(nc, [arrays], core_ids=[0])
    return r.results[0]["out_0"]
```
